# Optimizing a Trainium2 kernel written in Bass

```python
import numpy as np
import jax
import jax.numpy as jnp

def _softmax(x, axis=-1):
    return jax.nn.softmax(x, axis=axis)

def _gelu(x):
    return jax.nn.gelu(x, approximate=True)

def _silu(x):
    return jax.nn.silu(x)

def _sigmoid(x):
    return jax.nn.sigmoid(x)

def _layernorm(x, axis=-1, eps=1e-05):
    m = jnp.mean(x, axis=axis, keepdims=True)
    v = jnp.var(x, axis=axis, keepdims=True)
    return (x - m) / jnp.sqrt(v + eps)

def _scatter_add(tgt, idx, src, axis=0):
    return tgt.at[idx].add(src)

def _segment_sum(src, seg, n):
    return jax.ops.segment_sum(src, seg, n)
kernel_name = 'mk_xattn_seq_d4_seqx_r8_0dcd55'

def setup_inputs(seed: int=0):
    np.random.seed(seed)
    _w = jnp.asarray

    def _rec_inputs():
        import jax
        import jax.numpy as jnp
        _rk = jax.random.key(seed)
        x = -0.000719 + 1.001 * jax.random.normal(jax.random.fold_in(_rk, 1), (4, 256, 160), jnp.float32)
        _lenS = 256 - jax.random.randint(jax.random.fold_in(_rk, 7), (4,), 0, max(1, 256 // 4) + 1, jnp.int32)
        _lenS2 = 256 - jax.random.randint(jax.random.fold_in(_rk, 8), (4,), 0, max(1, 256 // 4) + 1, jnp.int32)
        _ctx_2048P = jax.random.normal(jax.random.fold_in(_rk, 11), (4, 16, 256), jnp.float32)
        _ctx_2048c = jax.random.dirichlet(jax.random.fold_in(_rk, 511), 0.3 * jnp.ones((16,), jnp.float32), (4, 256))
        _ctx_2048t = jnp.einsum('bsk,bkd->bsd', _ctx_2048c, _ctx_2048P)
        _ctx_2048t = _ctx_2048t * jax.lax.rsqrt(jnp.mean(jnp.square(_ctx_2048t)) + 1e-12) * 0.953939
        ctx_2048 = 0.00257118 + 0.99863 * (_ctx_2048t + 0.3 * jax.random.normal(jax.random.fold_in(_rk, 611), (4, 256, 256), jnp.float32))
        fside_S_0 = jax.random.uniform(jax.random.fold_in(_rk, 12), (256,), jnp.float32, 0.0, 0.999706)
        return (x, ctx_2048, fside_S_0)
    x, ctx_2048, fside_S_0 = _rec_inputs()

    def _L0_xattn_setup():
        import jax, jax.numpy as jnp
        import numpy as np
        HEADS = 20
        NUM_TOKENS = 4
        IP_SCALE = 1.0
        SEM_SCALE = 0.5
        RESCALE = 1.0
        EPS = 1e-12

        def _l2norm(x, axis=-1):
            n = jnp.sqrt(jnp.sum(x * x, axis=axis, keepdims=True))
            return x / jnp.maximum(n, EPS)
        key = jax.random.key(seed)
        ks = jax.random.split(key, 10)
        B, S, C = (2, 128, 160)
        T, E = (81, 256)
        inp = {'hidden_states': jax.random.normal(ks[0], (B, S, C), jnp.float32), 'encoder_hidden_states': jax.random.normal(ks[1], (B, T, E), jnp.float32), 'spatial_mask': jax.random.uniform(ks[2], (S,), jnp.float32), 'W_q': jax.random.normal(ks[3], (C, C), jnp.float32) * C ** (-0.5), 'W_k': jax.random.normal(ks[4], (E, C), jnp.float32) * E ** (-0.5), 'W_v': jax.random.normal(ks[5], (E, C), jnp.float32) * E ** (-0.5), 'W_k_ip': jax.random.normal(ks[6], (E, C), jnp.float32) * E ** (-0.5), 'W_v_ip': jax.random.normal(ks[7], (E, C), jnp.float32) * E ** (-0.5), 'W_out': jax.random.normal(ks[8], (C, C), jnp.float32) * C ** (-0.5), 'b_out': jnp.zeros((C,), jnp.float32)}
        return inp
    _L0_xattn_all = _L0_xattn_setup()
    _L0_xattn_in = {k: v for k, v in _L0_xattn_all.items() if k in ('W_q', 'W_k', 'W_v', 'W_k_ip', 'W_v_ip', 'W_out', 'b_out')}
    del _L0_xattn_all

    def _L1_xattn_setup():
        import jax, jax.numpy as jnp
        import numpy as np
        import math
        HEADS = 20
        NUM_TOKENS = 4
        SEM_SCALE = 0.5
        IP_SCALE = 1.0
        TEXT_LEN = 77

        def _split_heads(x, B, H, D):
            return x.reshape(B, -1, H, D).transpose(0, 2, 1, 3)
        key = jax.random.key(seed)
        ks = jax.random.split(key, 10)
        B, S, C, CD = (4, 512, 160, 256)

        def g(k, shape, std=1.0):
            return jax.random.normal(k, shape, dtype=jnp.float32) * std
        return {'hidden_states': g(ks[0], (B, S, C)), 'encoder_hidden_states': g(ks[1], (B, TEXT_LEN + NUM_TOKENS, CD)), 'spatial_mask': jax.random.uniform(ks[2], (S,), dtype=jnp.float32), 'Wq': g(ks[3], (C, C), 1.0 / math.sqrt(C)), 'Wk': g(ks[4], (CD, C), 1.0 / math.sqrt(CD)), 'Wv': g(ks[5], (CD, C), 1.0 / math.sqrt(CD)), 'Wk_ip': g(ks[6], (CD, C), 1.0 / math.sqrt(CD)), 'Wv_ip': g(ks[7], (CD, C), 1.0 / math.sqrt(CD)), 'Wout': g(ks[8], (C, C), 1.0 / math.sqrt(C)), 'bout': jnp.zeros((C,), dtype=jnp.float32)}
    _L1_xattn_all = _L1_xattn_setup()
    _L1_xattn_in = {k: v for k, v in _L1_xattn_all.items() if k in ('Wq', 'Wk', 'Wv', 'Wk_ip', 'Wv_ip', 'Wout', 'bout')}
    del _L1_xattn_all

    def _L2_xattn_setup():
        import jax, jax.numpy as jnp
        import numpy as np
        NUM_HEADS = 20
        TEXT_LEN = 77
        IP_SCALE = 1.0

        def _attend(q, k, v, sm_scale):
            scores = jnp.einsum('bhsd,bhld->bhsl', q, k) * sm_scale
            probs = jax.nn.softmax(scores, axis=-1)
            return jnp.einsum('bhsl,bhld->bhsd', probs, v)

        def _split_heads(x, h):
            b, s, c = x.shape
            return x.reshape(b, s, h, c // h).transpose(0, 2, 1, 3)

        def _merge_heads(x):
            b, h, s, d = x.shape
            return x.transpose(0, 2, 1, 3).reshape(b, s, h * d)
        key = jax.random.key(seed)
        ks = jax.random.split(key, 8)
        B, S, C, CC, L = (8, 512, 160, 256, TEXT_LEN + 4)
        sd_q = 1.0 / np.sqrt(C)
        sd_kv = 1.0 / np.sqrt(CC)
        return {'hidden_states': jax.random.normal(ks[0], (B, S, C), jnp.float32), 'encoder_hidden_states': jax.random.normal(ks[1], (B, L, CC), jnp.float32), 'Wq': jax.random.normal(ks[2], (C, C), jnp.float32) * sd_q, 'Wk': jax.random.normal(ks[3], (C, CC), jnp.float32) * sd_kv, 'Wv': jax.random.normal(ks[4], (C, CC), jnp.float32) * sd_kv, 'Wk_ip': jax.random.normal(ks[5], (C, CC), jnp.float32) * sd_kv, 'Wv_ip': jax.random.normal(ks[6], (C, CC), jnp.float32) * sd_kv, 'Wo': jax.random.normal(ks[7], (C, C), jnp.float32) * sd_q, 'bo': jnp.zeros((C,), jnp.float32)}
    _L2_xattn_all = _L2_xattn_setup()
    _L2_xattn_in = {k: v for k, v in _L2_xattn_all.items() if k in ('Wq', 'Wk', 'Wv', 'Wk_ip', 'Wv_ip', 'Wo', 'bo')}
    del _L2_xattn_all

    def _L3_xattn_setup():
        import jax, jax.numpy as jnp
        import numpy as np
        B, S, C = (2, 512, 160)
        CA = 256
        HEADS = 20
        HD = C // HEADS
        N_TXT, N_OBJ, N_OTH, N_IP = (77, 4, 4, 16)
        SCALE_OBJ = SCALE_OTH = SCALE_IP = 1.0
        RESCALE = 1.0

        def _heads(x):
            b, l, _ = x.shape
            return x.reshape(b, l, HEADS, HD).transpose(0, 2, 1, 3)

        def _merge(x):
            b, h, l, d = x.shape
            return x.transpose(0, 2, 1, 3).reshape(b, l, h * d)

        def _sdpa(q, k, v):
            scale = 1.0 / np.sqrt(HD).astype(np.float32)
            s = jnp.einsum('bhqd,bhkd->bhqk', q, k) * scale
            p = jax.nn.softmax(s, axis=-1)
            return jnp.einsum('bhqk,bhkd->bhqd', p, v)
        key = jax.random.key(seed)
        ks = jax.random.split(key, 16)
        g = lambda k, shp, fan: jax.random.normal(k, shp, jnp.float32) / np.sqrt(fan).astype(np.float32)
        return {'hidden_states': jax.random.normal(ks[0], (B, S, C), jnp.float32), 'encoder_hidden_states': jax.random.normal(ks[1], (B, N_TXT + N_OBJ + N_OTH + N_IP, CA), jnp.float32), 'to_q_w': g(ks[2], (C, C), C), 'to_k_w': g(ks[3], (CA, C), CA), 'to_v_w': g(ks[4], (CA, C), CA), 'to_k_object_w': g(ks[5], (CA, C), CA), 'to_v_object_w': g(ks[6], (CA, C), CA), 'to_k_others_w': g(ks[7], (CA, C), CA), 'to_v_others_w': g(ks[8], (CA, C), CA), 'to_k_ip_w': g(ks[9], (CA, C), CA), 'to_v_ip_w': g(ks[10], (CA, C), CA), 'to_out_w': g(ks[11], (C, C), C), 'to_out_b': jnp.zeros((C,), jnp.float32)}
    _L3_xattn_all = _L3_xattn_setup()
    _L3_xattn_in = {k: v for k, v in _L3_xattn_all.items() if k in ('to_q_w', 'to_k_w', 'to_v_w', 'to_k_object_w', 'to_v_object_w', 'to_k_others_w', 'to_v_others_w', 'to_k_ip_w', 'to_v_ip_w', 'to_out_w', 'to_out_b')}
    del _L3_xattn_all
    return {'x': x, 'ctx_2048': ctx_2048, 'fside_S_0': fside_S_0, 'L0_xattn_W_q': _L0_xattn_in['W_q'], 'L0_xattn_W_k': _L0_xattn_in['W_k'], 'L0_xattn_W_v': _L0_xattn_in['W_v'], 'L0_xattn_W_k_ip': _L0_xattn_in['W_k_ip'], 'L0_xattn_W_v_ip': _L0_xattn_in['W_v_ip'], 'L0_xattn_W_out': _L0_xattn_in['W_out'], 'L0_xattn_b_out': _L0_xattn_in['b_out'], 'L1_xattn_Wq': _L1_xattn_in['Wq'], 'L1_xattn_Wk': _L1_xattn_in['Wk'], 'L1_xattn_Wv': _L1_xattn_in['Wv'], 'L1_xattn_Wk_ip': _L1_xattn_in['Wk_ip'], 'L1_xattn_Wv_ip': _L1_xattn_in['Wv_ip'], 'L1_xattn_Wout': _L1_xattn_in['Wout'], 'L1_xattn_bout': _L1_xattn_in['bout'], 'L2_xattn_Wq': _L2_xattn_in['Wq'], 'L2_xattn_Wk': _L2_xattn_in['Wk'], 'L2_xattn_Wv': _L2_xattn_in['Wv'], 'L2_xattn_Wk_ip': _L2_xattn_in['Wk_ip'], 'L2_xattn_Wv_ip': _L2_xattn_in['Wv_ip'], 'L2_xattn_Wo': _L2_xattn_in['Wo'], 'L2_xattn_bo': _L2_xattn_in['bo'], 'L3_xattn_to_q_w': _L3_xattn_in['to_q_w'], 'L3_xattn_to_k_w': _L3_xattn_in['to_k_w'], 'L3_xattn_to_v_w': _L3_xattn_in['to_v_w'], 'L3_xattn_to_k_object_w': _L3_xattn_in['to_k_object_w'], 'L3_xattn_to_v_object_w': _L3_xattn_in['to_v_object_w'], 'L3_xattn_to_k_others_w': _L3_xattn_in['to_k_others_w'], 'L3_xattn_to_v_others_w': _L3_xattn_in['to_v_others_w'], 'L3_xattn_to_k_ip_w': _L3_xattn_in['to_k_ip_w'], 'L3_xattn_to_v_ip_w': _L3_xattn_in['to_v_ip_w'], 'L3_xattn_to_out_w': _L3_xattn_in['to_out_w'], 'L3_xattn_to_out_b': _L3_xattn_in['to_out_b']}

def reference(x, ctx_2048, fside_S_0, L0_xattn_W_q, L0_xattn_W_k, L0_xattn_W_v, L0_xattn_W_k_ip, L0_xattn_W_v_ip, L0_xattn_W_out, L0_xattn_b_out, L1_xattn_Wq, L1_xattn_Wk, L1_xattn_Wv, L1_xattn_Wk_ip, L1_xattn_Wv_ip, L1_xattn_Wout, L1_xattn_bout, L2_xattn_Wq, L2_xattn_Wk, L2_xattn_Wv, L2_xattn_Wk_ip, L2_xattn_Wv_ip, L2_xattn_Wo, L2_xattn_bo, L3_xattn_to_q_w, L3_xattn_to_k_w, L3_xattn_to_v_w, L3_xattn_to_k_object_w, L3_xattn_to_v_object_w, L3_xattn_to_k_others_w, L3_xattn_to_v_others_w, L3_xattn_to_k_ip_w, L3_xattn_to_v_ip_w, L3_xattn_to_out_w, L3_xattn_to_out_b):
    import jax
    import jax.numpy as jnp

    def _L0_xattn_ref(hidden_states, encoder_hidden_states, spatial_mask, W_q, W_k, W_v, W_k_ip, W_v_ip, W_out, b_out):
        import jax, jax.numpy as jnp
        import numpy as np
        HEADS = 20
        NUM_TOKENS = 4
        IP_SCALE = 1.0
        SEM_SCALE = 0.5
        RESCALE = 1.0
        EPS = 1e-12

        def _l2norm(x, axis=-1):
            n = jnp.sqrt(jnp.sum(x * x, axis=axis, keepdims=True))
            return x / jnp.maximum(n, EPS)
        B, S, C = hidden_states.shape
        H = HEADS
        Dh = C // H
        attn_scale = Dh ** (-0.5)
        residual = hidden_states
        text_ehs = encoder_hidden_states[:, :-NUM_TOKENS]
        ip_ehs = encoder_hidden_states[:, -NUM_TOKENS:]

        def heads(x):
            return x.reshape(B, -1, H, Dh).transpose(0, 2, 1, 3)
        q = heads(hidden_states @ W_q)
        k_t = heads(text_ehs @ W_k)
        v_t = heads(text_ehs @ W_v)
        scores_t = jnp.einsum('bhsd,bhtd->bhst', q, k_t) * attn_scale
        probs_t = jax.nn.softmax(scores_t, axis=-1)
        text_out = jnp.einsum('bhst,bhtd->bhsd', probs_t, v_t)
        text_out = text_out.transpose(0, 2, 1, 3).reshape(B, S, C)
        k_ip = heads(ip_ehs @ W_k_ip)
        v_ip = heads(ip_ehs @ W_v_ip)
        attn_scores = jnp.einsum('bhsd,bhnd->bhsn', q, k_ip) * attn_scale
        qsem = jnp.einsum('bhst,bte->bhse', probs_t, text_ehs)
        qsem = _l2norm(qsem)
        ip_n = _l2norm(ip_ehs)
        sem = jnp.einsum('bhse,bne->bhsn', qsem, ip_n)
        sem = jax.lax.stop_gradient(sem)
        fused = attn_scores + SEM_SCALE * sem
        probs_ip = jax.nn.softmax(fused, axis=-1)
        probs_ip = probs_ip * spatial_mask[None, None, :, None]
        ip_out = jnp.einsum('bhsn,bhnd->bhsd', probs_ip, v_ip)
        ip_out = ip_out.transpose(0, 2, 1, 3).reshape(B, S, C)
        out = text_out + IP_SCALE * ip_out
        out = out @ W_out + b_out
        out = out + residual
        return out / RESCALE

    def _L1_xattn_ref(hidden_states, encoder_hidden_states, spatial_mask, Wq, Wk, Wv, Wk_ip, Wv_ip, Wout, bout):
        import jax, jax.numpy as jnp
        import numpy as np
        import math
        HEADS = 20
        NUM_TOKENS = 4
        SEM_SCALE = 0.5
        IP_SCALE = 1.0
        TEXT_LEN = 77

        def _split_heads(x, B, H, D):
            return x.reshape(B, -1, H, D).transpose(0, 2, 1, 3)
        B, S, C = hidden_states.shape
        D = C // HEADS
        scale = 1.0 / math.sqrt(D)
        residual = hidden_states
        text = encoder_hidden_states[:, :TEXT_LEN]
        ip = encoder_hidden_states[:, TEXT_LEN:]
        q = hidden_states @ Wq
        k_text = text @ Wk
        v_text = text @ Wv
        q_h = _split_heads(q, B, HEADS, D)
        k_h = _split_heads(k_text, B, HEADS, D)
        v_h = _split_heads(v_text, B, HEADS, D)
        logits = jnp.einsum('bhqd,bhkd->bhqk', q_h, k_h) * scale
        probs = jax.nn.softmax(logits, axis=-1)
        text_out = jnp.einsum('bhqk,bhkd->bhqd', probs, v_h)
        text_out = text_out.transpose(0, 2, 1, 3).reshape(B, S, C)
        ip_k = ip @ Wk_ip
        ip_v = ip @ Wv_ip
        ip_k_h = _split_heads(ip_k, B, HEADS, D)
        ip_v_h = _split_heads(ip_v, B, HEADS, D)
        scores = jnp.einsum('bhqd,bhkd->bhqk', q_h, ip_k_h) * scale
        text_probs = jax.nn.softmax(jnp.einsum('bqc,bkc->bqk', q, k_text) * scale, axis=-1)
        q_sem = jnp.einsum('bqk,bkc->bqc', text_probs, text)
        sem = jnp.einsum('bqc,bnc->bqn', q_sem, ip) * scale
        sem = jax.lax.stop_gradient(sem)
        fused = scores + SEM_SCALE * sem[:, None, :, :]
        ip_probs = jax.nn.softmax(fused, axis=-1)
        ip_probs = ip_probs * spatial_mask[None, None, :, None]
        ip_out = jnp.einsum('bhqk,bhkd->bhqd', ip_probs, ip_v_h)
        ip_out = ip_out.transpose(0, 2, 1, 3).reshape(B, S, C)
        hs = text_out + IP_SCALE * ip_out
        out = hs @ Wout + bout
        out = out + residual
        return out

    def _L2_xattn_ref(hidden_states, encoder_hidden_states, Wq, Wk, Wv, Wk_ip, Wv_ip, Wo, bo):
        import jax, jax.numpy as jnp
        import numpy as np
        NUM_HEADS = 20
        TEXT_LEN = 77
        IP_SCALE = 1.0

        def _attend(q, k, v, sm_scale):
            scores = jnp.einsum('bhsd,bhld->bhsl', q, k) * sm_scale
            probs = jax.nn.softmax(scores, axis=-1)
            return jnp.einsum('bhsl,bhld->bhsd', probs, v)

        def _split_heads(x, h):
            b, s, c = x.shape
            return x.reshape(b, s, h, c // h).transpose(0, 2, 1, 3)

        def _merge_heads(x):
            b, h, s, d = x.shape
            return x.transpose(0, 2, 1, 3).reshape(b, s, h * d)
        residual = hidden_states
        B, S, C = hidden_states.shape
        H = NUM_HEADS
        D = C // H
        sm_scale = 1.0 / jnp.sqrt(jnp.asarray(D, hidden_states.dtype))
        text = encoder_hidden_states[:, :TEXT_LEN, :]
        ip = encoder_hidden_states[:, TEXT_LEN:, :]
        q = _split_heads(hidden_states @ Wq.T, H)
        k = _split_heads(text @ Wk.T, H)
        v = _split_heads(text @ Wv.T, H)
        out_text = _merge_heads(_attend(q, k, v, sm_scale))
        k_ip = _split_heads(ip @ Wk_ip.T, H)
        v_ip = _split_heads(ip @ Wv_ip.T, H)
        out_ip = _merge_heads(_attend(q, k_ip, v_ip, sm_scale))
        out = out_text + IP_SCALE * out_ip
        out = out @ Wo.T + bo
        return out + residual

    def _L3_xattn_ref(hidden_states, encoder_hidden_states, to_q_w, to_k_w, to_v_w, to_k_object_w, to_v_object_w, to_k_others_w, to_v_others_w, to_k_ip_w, to_v_ip_w, to_out_w, to_out_b):
        import jax, jax.numpy as jnp
        import numpy as np
        B, S, C = (2, 512, 160)
        CA = 256
        HEADS = 20
        HD = C // HEADS
        N_TXT, N_OBJ, N_OTH, N_IP = (77, 4, 4, 16)
        SCALE_OBJ = SCALE_OTH = SCALE_IP = 1.0
        RESCALE = 1.0

        def _heads(x):
            b, l, _ = x.shape
            return x.reshape(b, l, HEADS, HD).transpose(0, 2, 1, 3)

        def _merge(x):
            b, h, l, d = x.shape
            return x.transpose(0, 2, 1, 3).reshape(b, l, h * d)

        def _sdpa(q, k, v):
            scale = 1.0 / np.sqrt(HD).astype(np.float32)
            s = jnp.einsum('bhqd,bhkd->bhqk', q, k) * scale
            p = jax.nn.softmax(s, axis=-1)
            return jnp.einsum('bhqk,bhkd->bhqd', p, v)
        residual = hidden_states
        end = N_TXT
        ehs_txt = encoder_hidden_states[:, :end]
        ehs_obj = encoder_hidden_states[:, end:end + N_OBJ]
        ehs_oth = encoder_hidden_states[:, end + N_OBJ:end + N_OBJ + N_OTH]
        ehs_ip = encoder_hidden_states[:, end + N_OBJ + N_OTH:]
        q = _heads(hidden_states @ to_q_w)
        h_txt = _sdpa(q, _heads(ehs_txt @ to_k_w), _heads(ehs_txt @ to_v_w))
        h_obj = _sdpa(q, _heads(ehs_obj @ to_k_object_w), _heads(ehs_obj @ to_v_object_w))
        h_oth = _sdpa(q, _heads(ehs_oth @ to_k_others_w), _heads(ehs_oth @ to_v_others_w))
        h_ip = _sdpa(q, _heads(ehs_ip @ to_k_ip_w), _heads(ehs_ip @ to_v_ip_w))
        out = _merge(h_txt) + SCALE_OBJ * _merge(h_obj) + SCALE_OTH * _merge(h_oth) + SCALE_IP * _merge(h_ip)
        out = out @ to_out_w + to_out_b
        out = (out + residual) / RESCALE
        return out
    x = _L0_xattn_ref(x, ctx_2048, fside_S_0, L0_xattn_W_q, L0_xattn_W_k, L0_xattn_W_v, L0_xattn_W_k_ip, L0_xattn_W_v_ip, L0_xattn_W_out, L0_xattn_b_out)
    x = _L1_xattn_ref(x, ctx_2048, fside_S_0, L1_xattn_Wq, L1_xattn_Wk, L1_xattn_Wv, L1_xattn_Wk_ip, L1_xattn_Wv_ip, L1_xattn_Wout, L1_xattn_bout)
    x = _L2_xattn_ref(x, ctx_2048, L2_xattn_Wq, L2_xattn_Wk, L2_xattn_Wv, L2_xattn_Wk_ip, L2_xattn_Wv_ip, L2_xattn_Wo, L2_xattn_bo)
    x = _L3_xattn_ref(x, ctx_2048, L3_xattn_to_q_w, L3_xattn_to_k_w, L3_xattn_to_v_w, L3_xattn_to_k_object_w, L3_xattn_to_v_object_w, L3_xattn_to_k_others_w, L3_xattn_to_v_others_w, L3_xattn_to_k_ip_w, L3_xattn_to_v_ip_w, L3_xattn_to_out_w, L3_xattn_to_out_b)
    return x

_drawn_inputs = setup_inputs


def setup_inputs(seed=0):
    import zlib

    import numpy as np

    out = dict(_drawn_inputs(seed))
    spreads = {'L0_xattn_b_out': (0.0, 0.1),
     'L1_xattn_bout': (0.0, 0.1),
     'L2_xattn_bo': (0.0, 0.1),
     'L3_xattn_to_out_b': (0.0, 0.1)}
    factors = {}
    for name, (base, spread) in spreads.items():
        noise = np.random.default_rng([zlib.crc32(name.encode()), seed]).standard_normal(out[name].shape)
        drawn = base * np.exp(spread * noise) if base else spread * noise
        out[name] = jnp.asarray(drawn.astype(out[name].dtype))
    for name, factor in factors.items():
        out[name] = (out[name] * factor).astype(out[name].dtype)
    return out
```

```python
from contextlib import ExitStack

import concourse.bass as bass
from concourse import mybir

F32 = mybir.dt.float32
BF16 = mybir.dt.bfloat16
ACT = mybir.ActivationFunctionType
ALU = mybir.AluOpType
AX = mybir.AxisListType

P = 128
B, S, C, E, T = 4, 256, 160, 256, 256
H, D = 20, 8
NL = 4
SLOTS = NL * B
SCALE = float(D) ** -0.5
HALF = C // 2
QUADS = H // 4
NS = H // 2
NPROD = 6
ROWS = NPROD * D
QT = S // P
KT = T // P
EPS2 = 1e-24

SEGS = [
    [(0, 252), (252, 256)],
    [(0, 77), (77, 256)],
    [(0, 77), (77, 256)],
    [(0, 77), (77, 81), (81, 85), (85, 256)],
]
NTEXT = 77
PATTERN = [0, 1, 1, 2]
HROWS = [32, 32, 32, 64]
NIP0 = 4


def layer(s):
    return s // B


def batch(s):
    return s % B


def v_parts(l):
    segs = SEGS[l][:1] if l == 0 else SEGS[l]
    pairs = [(c, g) for c in range(KT) for g, (a, z) in enumerate(segs) if a < (c + 1) * P and z > c * P]
    return [pairs[i:i + 3] for i in range(0, len(pairs), 3)]


def t_rounds(l):
    units = H * HROWS[l] // P
    n = 3 if l < 3 else 4
    return [list(range(i, min(i + n, units))) for i in range(0, units, n)]


def early_rounds(l):
    return 1


def hops(s):
    at = [[] for _ in range(6)]
    if 0 <= s + 3 < SLOTS:
        at[0].append(("K", s + 3))
    if 0 <= s - 1 < SLOTS:
        l = layer(s - 1)
        for n in range(early_rounds(l), len(t_rounds(l))):
            for qt in range(QT):
                at[0].append(("T", s - 1, n, qt))
        at[1].append(("AT", s - 1))
        at[2].append(("OUT", s - 1))
    if 0 <= s + 1 < SLOTS:
        at[0].append(("M", s + 1))
    if 0 <= s + 3 < SLOTS:
        at[3].append(("Q", s + 3))
    if 0 <= s < SLOTS:
        for n in range(early_rounds(layer(s))):
            for qt in range(QT):
                at[4].append(("T", s, n, qt))
    if 0 <= s + 3 < SLOTS and layer(s + 3) == 1:
        at[5].append(("FULL", s + 3))
    if 0 <= s + 1 < SLOTS:
        l = layer(s + 1)
        for n in range(len(v_parts(l))):
            at[5].append(("V", s + 1, n))
        if l == 0:
            at[5] += [("VIP", s + 1, 0), ("VIP", s + 1, 1)]
    if 0 <= s + 3 < SLOTS and layer(s + 3) == 1:
        at[5] += [("PT", s + 3), ("SEM", s + 3), ("SEMT", s + 3)]
    return at


FIRST, LAST = -3, SLOTS


def hop_banks(s):
    return [5] if 0 <= s < B else [5, 6]


def score_banks(s):
    return [2, 3] if s < B else [2, 3, 7]


class Plan:

    def __init__(self):
        self.hop, n, used = {}, 0, {5: 0, 6: 0}
        self.hop[("NORM",)] = (0, 5, 0)
        n, used[5] = 1, 1
        for s in range(FIRST, LAST + 1):
            for pos in hops(s):
                for key in pos:
                    bank = hop_banks(s)[n % len(hop_banks(s))]
                    self.hop[key] = (n, bank, used[bank])
                    used[bank] += 1
                    n += 1
        on6 = [(n, k, used) for k, (n, bank, used) in self.hop.items() if bank == 6]
        start = self.hop[("K", 3)][0]
        self.hops_on_6_before_text = sum(1 for n, _, _ in on6 if n < start)
        self.first_on_6_after_text = min((n, k) for n, k, _ in on6 if n > start)[1]
        self.unit, last, n = {}, {}, 0
        for a in range(SLOTS):
            for j in range(QUADS):
                for u in range(4):
                    banks = score_banks(a - 2)
                    bank = banks[n % len(banks)]
                    self.unit[(a, j, u)] = (n, bank, last.get(bank))
                    last[bank] = n
                    n += 1
        self.split, n = {}, 0
        for s in range(FIRST, LAST + 1):
            for pos in hops(s):
                for key in pos:
                    if key[0] in ("K", "Q", "SEM", "SEMT"):
                        self.split[key] = n
                        n += 1


def program(nc, t):
    plan = Plan()
    with ExitStack() as ctx:
        def sb(name, shape, dt=F32):
            return ctx.enter_context(nc.sbuf_tensor(name, shape, dt))

        def sem(name):
            return ctx.enter_context(nc.semaphore(name))

        bank = [ctx.enter_context(nc.psum_tensor(f"bank{i}", [P, 512], F32)) for i in range(8)]

        xT = sb("xT", [HALF, 2, B * S])
        ctxT = sb("ctxT", [P, 2, B * T])
        text = sb("text", [P, B * KT, E])
        wq = sb("wq", [HALF, NL, 2, C])
        wo = sb("wo", [HALF, NL, 2, C])
        bo = sb("bo", [HALF, NL, 2])
        wk = [sb(f"wk{l}", [P, len(SEGS[l]), 2, C]) for l in range(NL)]
        wv = [sb(f"wv{l}", [P, len(SEGS[l]), 2, C]) for l in range(NL)]
        spatial = sb("spatial", [P, QT])
        segmask = sb("segmask", [P, 3, KT, 4])
        ident = sb("ident", [P, P])
        identb = sb("identb", [P, P], BF16)
        ones = sb("ones", [P, P])
        kstack = sb("kstack", [P, 4, NS, T], BF16)
        qstack = sb("qstack", [P, 4, NS, S], BF16)
        ksplit = sb("ksplit", [HALF, 3, 2, T], BF16)
        qsplit = sb("qsplit", [HALF, 3, 2, S], BF16)
        rest = sb("rest", [P, 1, 512])
        negmax = sb("negmax", [P, 2, QT, 4 * H])
        maxrest = sb("maxrest", [P, QT, 4 * H])
        maxsplit = sb("maxsplit", [P, QT, 3, 4 * H], BF16)
        maxT = sb("maxT", [120, 2, S], BF16)
        probs = sb("probs", [P, 8, KT, S])
        vals_wide = sb("vals_wide", [P, 2, KT, H, 64])
        vals_mid = sb("vals_mid", [P, 2, KT, H, 32])
        vals = [vals_wide[:, :, :, :, 0:32], vals_mid[:], vals_wide[:]]
        outT = sb("outT", [P, H // 2, S])
        rsum = sb("rsum", [P, QT, H, 4])
        scaled = sb("scaled", [P, 12, 4, D])
        attn = sb("attn", [P, QT, C])
        attnT = sb("attnT", [HALF, 2, S])
        s_ip = sb("s_ip", [P, 4, QT, H, NIP0])
        norm2 = sb("norm2", [P, 2, QT, H])
        dots = sb("dots", [P, QT, H, NIP0])
        ipsq = sb("ipsq", [P, 2, B, NIP0])
        ipn = sb("ipn", [P, 3, B, NIP0])
        v_ip = sb("v_ip", [P, 2, NIP0, C])
        nrm = sb("nrm", [P, 4, QT, H])
        fused = sb("fused", [P, 3, QT, H, NIP0])
        fsum = sb("fsum", [P, 5, QT, H])
        ipprod = sb("ipprod", [P, NIP0, C])
        ipout = sb("ipout", [P, C])
        qfull = sb("qfull", [HALF, 2, S])
        kfull = sb("kfull", [HALF, 2, NTEXT])
        textip = sb("textip", [NTEXT, T])
        pfull = sb("pfull", [P, 2, QT, NTEXT])
        fstat = sb("fstat", [P, 4, QT])
        pfullT = sb("pfullT", [NTEXT, S])
        semq = sb("semq", [P, 3, QT * T], BF16)
        semk = sb("semk", [P, 3, 3, KT * S], BF16)

        k_dram = nc.dram_tensor("k_dram", [SLOTS, 3, 2, HALF * T], BF16).ap()
        q_dram = nc.dram_tensor("q_dram", [SLOTS, 3, 2, HALF * S], BF16).ap()
        m_dram = nc.dram_tensor("m_dram", [SLOTS, 240, S], BF16).ap()

        loaded_x = sem("loaded_x")
        loaded_ctx = sem("loaded_ctx")
        loaded_wk = [sem(f"loaded_wk{l}") for l in range(NL)]
        loaded_w = [sem(f"loaded_w{l}") for l in range(NL)]
        loaded_const = sem("loaded_const")
        k_stored = sem("k_stored")
        q_stored = sem("q_stored")
        m_stored = sem("m_stored")
        k_loaded = [sem(f"k_loaded{i}") for i in range(4)]
        q_loaded = [sem(f"q_loaded{i}") for i in range(4)]
        m_loaded = [sem(f"m_loaded{i}") for i in range(4)]
        out_stored = sem("out_stored")
        st_full = sem("st_full")
        probs_ready = sem("probs_ready")
        s_full = sem("s_full")
        s_free = sem("s_free")
        o_full = sem("o_full")
        outT_ready = sem("outT_ready")
        y_full = sem("y_full")
        y_free = sem("y_free")
        hop_full = sem("hop_full")
        hop_taken = {5: sem("hop5_taken"), 6: sem("hop6_taken")}
        high_ready = sem("high_ready")
        rest_ready = sem("rest_ready")
        split_ready = sem("split_ready")
        maxsplit_ready = sem("maxsplit_ready")
        attn_ready = sem("attn_ready")
        full_ready = sem("full_ready")
        textip_ready = sem("textip_ready")
        bias_ready = sem("bias_ready")
        pfull_ready = sem("pfull_ready")
        norm_ready = sem("norm_ready")
        root_ready = sem("root_ready")
        fused_ready = sem("fused_ready")
        fexp_ready = sem("fexp_ready")
        text_masked = sem("text_masked")
        ipsq_ready = sem("ipsq_ready")
        vals_zeroed = sem("vals_zeroed")
        vals_marked = sem("vals_marked")
        ones_ready = sem("ones_ready")
        dve_step = sem("dve_step")
        pool_step = sem("pool_step")
        block = ctx.enter_context(nc.Block())

        def heads_of(unit):
            return unit // 2, unit % 2

        def full_of(key):
            return plan.hop[key][0] + 1

        def hop_view(key):
            return bank[plan.hop[key][1]]

        def tr_view(l, key, units):
            r = HROWS[l]
            return hop_view(key)[:, 0:len(units) * P].rearrange("p (h r) -> p h r", r=r)

        def taken(eng, key):
            _, b, before = plan.hop[key]
            eng.wait_ge(hop_taken[b], before + 1)

        def last_values_hop(s):
            return ("V", s, len(v_parts(layer(s))) - 1)

        def st_count(s, h):
            return s * H + h + 1

        def quad_heads(j):
            return range(4 * j, 4 * j + 4)

        def k_dmas(s):
            return 8 if s < B or PATTERN[layer(s)] != PATTERN[layer(s) - 1] else 6

        def k_loaded_count(s):
            return 16 * sum(k_dmas(x) for x in range(batch(s), s + 1, B))

        @block.sync
        def _(sp):
            sp.dma_start(ctxT[:], t["ctxT"]).then_inc(loaded_ctx, 16)
            sp.dma_start(wk[0][:], t["wk0"]).then_inc(loaded_wk[0], 16)
            sp.dma_start(xT[:], t["xT"]).then_inc(loaded_x, 16)
            for name, dst in (("segmask", segmask), ("ident", ident), ("identb", identb), ("spatial", spatial),
                              ("text", text), ("wq", wq), ("wo", wo), ("bo", bo)):
                sp.dma_start(dst[:], t[name]).then_inc(loaded_const, 16)
            sp.dma_start(wv[0][:], t["wv0"]).then_inc(loaded_w[0], 16)
            for l in range(1, NL):
                sp.dma_start(wk[l][:], t[f"wk{l}"]).then_inc(loaded_wk[l], 16)
                sp.dma_start(wv[l][:], t[f"wv{l}"]).then_inc(loaded_w[l], 16)

            def stack(dst, src, order, done):
                for half in range(2):
                    for row, n, part, step in order:
                        a = src[part:part + (n if step else 1), half, :].rearrange("r (d x) -> r d x", d=D)
                        if not step and n > 1:
                            a = a.broadcast_to([n, D, NS * T])
                        sp.dma_start(dst[64 * half + row * D:64 * half + (row + n) * D, :], a).then_inc(done, 16)

            for s in range(FIRST, LAST):
                k = s + 3
                if k < SLOTS:
                    if k >= B:
                        sp.wait_ge(st_full, st_count(k - B, H - 1))
                    sp.wait_ge(split_ready, plan.split[("K", k)] + 1)
                    sp.dma_start(k_dram[k].rearrange("a h (p t) -> p (a h) t", p=HALF),
                                 ksplit[:].rearrange("p a h t -> p (a h) t")).then_inc(k_stored, 16)
                if 0 <= s + 1 < SLOTS:
                    m = s + 1
                    nblk = len(SEGS[layer(m)]) * 3 * H // 120
                    taken(sp, ("M", m))
                    sp.dma_start(m_dram[m, 0:nblk * 120].rearrange("(n p) q -> p n q", n=nblk),
                                 maxT[:, 0:nblk, :]).then_inc(m_stored, 16)
                if k < SLOTS:
                    if k_dmas(k) == 8:
                        n = 3 * len(SEGS[layer(k)])
                        for half in range(2):
                            sp.dma_start(kstack[64 * half + ROWS:64 * half + ROWS + n, batch(k)]
                                         .rearrange("r s t -> r (s t)"),
                                         t[f"marks{PATTERN[layer(k)]}"]).then_inc(k_loaded[batch(k)], 16)
                    sp.wait_ge(k_stored, 16 * (k + 1))
                    stack(kstack[:, batch(k)].rearrange("r s t -> r (s t)"), k_dram[k],
                          ((0, 3, 0, 1), (3, 2, 0, 1), (5, 1, 0, 0)), k_loaded[batch(k)])
                if 0 <= s + 1 < SLOTS:
                    sp.wait_ge(m_stored, 16 * (m + 1))
                    n = 3 * len(SEGS[layer(m)])
                    for half in range(2):
                        sp.dma_start(qstack[64 * half + ROWS:64 * half + ROWS + n, batch(m)],
                                     m_dram[m, 0:n * H].rearrange("(r h s) q -> h r s q", h=2, s=NS)[half])\
                            .then_inc(m_loaded[batch(m)], 16)
                if s >= 1 and layer(s - 1) == NL - 1:
                    taken(sp, ("OUT", s - 1))
                    b = batch(s - 1)
                    sp.dma_start(t["out"][:, :, b * S:(b + 1) * S], xT[:, :, b * S:(b + 1) * S]).then_inc(out_stored, 16)
                if k < SLOTS:
                    sp.wait_ge(split_ready, plan.split[("Q", k)] + 1)
                    sp.dma_start(q_dram[k].rearrange("a h (p t) -> p (a h) t", p=HALF),
                                 qsplit[:].rearrange("p a h t -> p (a h) t")).then_inc(q_stored, 16)
                    sp.wait_ge(q_stored, 16 * (k + 1))
                    stack(qstack[:, batch(k)].rearrange("r s t -> r (s t)"), q_dram[k],
                          ((0, 3, 0, 0), (3, 2, 1, 0), (5, 1, 2, 0)), q_loaded[batch(k)])
            taken(sp, ("OUT", SLOTS - 1))
            b = B - 1
            sp.dma_start(t["out"][:, :, b * S:(b + 1) * S], xT[:, :, b * S:(b + 1) * S]).then_inc(out_stored, 16)
            sp.wait_ge(out_stored, 16 * B)

        @block.tensor
        def _(pe):
            mm = nc.tensor.matmul

            def begin(key):
                n, b, before = plan.hop[key]
                if before:
                    pe.wait_ge(hop_taken[b], before)
                if key == plan.first_on_6_after_text:
                    pe.wait_ge(y_free, B * H)
                return bank[b]

            def scores_for_max(a, j, u):
                qt, half = heads_of(u)
                n, b, last = plan.unit[(a, j, u)]
                if j == 0 and u == 0:
                    pe.wait_ge(k_loaded[batch(a)], k_loaded_count(a))
                    pe.wait_ge(q_loaded[batch(a)], 96 * (layer(a) + 1))
                if last is not None:
                    pe.wait_ge(s_free, last + 1)
                elif b == 7:
                    pe.wait_ge(y_free, B * H)
                r0 = 64 * half
                sem_add = layer(a) == 1
                out = bank[b]
                if sem_add:
                    if j == 0 and u == 0:
                        pe.wait_ge(split_ready, plan.split[("SEMT", a)] + 1)
                    for part in range(3):
                        mm(out[:].rearrange("p (s t) -> p s t", s=2), identb[:],
                           semq[:, part, qt * T:(qt + 1) * T].unsqueeze(1).broadcast_to([P, 2, T]),
                           start=(part == 0), stop=False)
                for i in range(2):
                    ins = mm(out[:, i * T:(i + 1) * T],
                             qstack[r0:r0 + ROWS, batch(a), 2 * j + i, qt * P:(qt + 1) * P],
                             kstack[r0:r0 + ROWS, batch(a), 2 * j + i, :],
                             start=not sem_add, stop=(not sem_add) or i == 1)
                ins.then_inc(s_full, 1)

            def scores_for_exp(s, h):
                if h == 0:
                    pe.wait_ge(m_loaded[batch(s)], 32 * (layer(s) + 1))
                n = s * H + h
                if n >= 2:
                    pe.wait_ge(probs_ready, n - 1)
                r0, rows = 64 * (h % 2), ROWS + 3 * len(SEGS[layer(s)])
                out = bank[n % 2]
                sem_add = layer(s) == 1
                if sem_add:
                    for part in range(3):
                        mm(out[:], identb[:], semk[:, s % 3, part, :], start=(part == 0), stop=False)
                for c in range(KT):
                    ins = mm(out[:, c * S:(c + 1) * S],
                             kstack[r0:r0 + rows, batch(s), h // 2, c * P:(c + 1) * P],
                             qstack[r0:r0 + rows, batch(s), h // 2, :],
                             start=not sem_add, stop=(not sem_add) or c == 1)
                ins.then_inc(st_full, 1)

            def values_product(s, j):
                l = layer(s)
                rows, buf = HROWS[l], vals[PATTERN[l]]
                if j == 0:
                    pe.wait_ge(vals_marked, 2 if l == 3 else 1)
                    taken(pe, last_values_hop(s))
                pe.wait_ge(probs_ready, st_count(s, 4 * j + 3))
                n = s * QUADS + j
                if n:
                    pe.wait_ge(outT_ready, n)
                per = P // rows
                for g in range(4 // per):
                    for c in range(KT):
                        for i in range(per):
                            h = 4 * j + g * per + i
                            ins = mm(bank[4][i * rows:(i + 1) * rows, g * S:(g + 1) * S],
                                     buf[:, s % 2, c, h, :], probs[:, h % 8, c, :],
                                     start=(c == 0), stop=(c == 1))
                ins.then_inc(o_full, 1)

            def text_product(s, j):
                for h in quad_heads(j):
                    n = s * H + h
                    if n >= 2:
                        pe.wait_ge(y_free, n - 1)
                    elif n == 0:
                        pe.wait_ge(hop_taken[6], plan.hops_on_6_before_text)
                    out = bank[6 + n % 2]
                    for qt in range(QT):
                        for c in range(KT):
                            ins = mm(out[:, qt * E:(qt + 1) * E], probs[:, h % 8, c, qt * P:(qt + 1) * P],
                                     text[:, KT * batch(s) + c, :], start=(c == 0), stop=(c == KT - 1))
                    ins.then_inc(y_full, 1)

            def project(out, w, src, cols):
                for half in range(2):
                    for k in range(2):
                        ins = mm(out[0:HALF, half * cols:(half + 1) * cols], w[:, k, half * HALF:(half + 1) * HALF],
                                 src[:, k, :], start=(k == 0), stop=(k == 1))
                return ins

            def hop(key):
                kind, s = key[0], key[1]
                l, b = layer(s), batch(s)
                if kind == "K":
                    if s < 1:
                        pe.wait_ge(loaded_ctx, 16)
                    if b == 0:
                        pe.wait_ge(loaded_wk[l], 16)
                    out = begin(key)
                    for half in range(2):
                        for g, (a, z) in enumerate(SEGS[l]):
                            for e in range(2):
                                ins = mm(out[0:HALF, half * T + a:half * T + z],
                                         wk[l][:, g, e, half * HALF:(half + 1) * HALF],
                                         ctxT[:, e, b * T + a:b * T + z], start=(e == 0), stop=(e == 1))
                elif kind == "Q":
                    if s == 0:
                        pe.wait_ge(loaded_x, 16)
                        pe.wait_ge(loaded_const, 16 * 8)
                    if s >= B:
                        taken(pe, ("OUT", s - B))
                    out = begin(key)
                    ins = project(out, wq[:, l], xT[:, :, b * S:(b + 1) * S], S)
                elif kind == "M":
                    pe.wait_ge(maxsplit_ready, s + 1)
                    out = begin(key)[:].bitcast(BF16)
                    n = 3 * len(SEGS[l]) * H
                    for qt in range(QT):
                        flat = maxsplit[:, qt].rearrange("p a n -> p (a n)")
                        for k in range(n // 120):
                            ins = nc.tensor.transpose(out[0:120, k * S + qt * P:k * S + (qt + 1) * P],
                                                      flat[:, k * 120:(k + 1) * 120], identb[:])
                elif kind == "T":
                    _, _, n, qt = key
                    units = t_rounds(l)[n]
                    per = 4 * HROWS[l] // P
                    pe.wait_ge(outT_ready, s * QUADS + units[-1] // per + 1)
                    out = begin(key)
                    for i, u in enumerate(units):
                        ins = nc.tensor.transpose(out[:, i * P:(i + 1) * P], outT[:, u, qt * P:(qt + 1) * P],
                                                  ident[:])
                elif kind == "AT":
                    pe.wait_ge(attn_ready, s + 1)
                    out = begin(key)
                    for half in range(2):
                        for qt in range(QT):
                            ins = nc.tensor.transpose(out[0:HALF, half * S + qt * P:half * S + (qt + 1) * P],
                                                      attn[:, qt, half * HALF:(half + 1) * HALF], ident[:])
                elif kind == "OUT":
                    taken(pe, ("AT", s))
                    out = begin(key)
                    ins = project(out, wo[:, l], attnT[:], S)
                elif kind == "V":
                    if b == 0:
                        pe.wait_ge(loaded_w[l], 16)
                    out = begin(key)
                    for i, (c, g) in enumerate(v_parts(l)[key[2]]):
                        for e in range(2):
                            ins = mm(out[:, i * C:(i + 1) * C], ctxT[:, e, b * T + c * P:b * T + (c + 1) * P],
                                     wv[l][:, g, e, :], start=(e == 0), stop=(e == 1))
                    if l == 0:
                        for c in range(KT):
                            for e in range(2):
                                ins = mm(out[:, 2 * C + c * NIP0:2 * C + (c + 1) * NIP0],
                                         ctxT[:, e, b * T + c * P:b * T + (c + 1) * P],
                                         ctxT[:, e, (b + 1) * T - NIP0:(b + 1) * T], start=(e == 0), stop=(e == 1))
                elif kind == "VIP":
                    out = begin(key)
                    for i in range(3 if key[2] == 0 else 1):
                        col = (b + 1) * T - NIP0 + 3 * key[2] + i
                        for e in range(2):
                            ins = mm(out[:, i * C:(i + 1) * C], ctxT[:, e, col:col + 1].broadcast_to([P, P]),
                                     wv[0][:, 1, e, :], start=(e == 0), stop=(e == 1))
                elif kind == "FULL":
                    out = begin(key)
                    for e in range(2):
                        mm(out[0:NTEXT, 0:T - NTEXT], ctxT[:, e, b * T:b * T + NTEXT],
                           ctxT[:, e, b * T + NTEXT:(b + 1) * T], start=(e == 0), stop=(e == 1))
                    pe.wait_ge(full_ready, 2 * (b + 1))
                    for qt in range(QT):
                        for k in range(2):
                            ins = mm(out[:, 256 + qt * NTEXT:256 + (qt + 1) * NTEXT], qfull[:, k, qt * P:(qt + 1) * P],
                                     kfull[:, k, :], start=(k == 0), stop=(k == 1))
                elif kind == "PT":
                    pe.wait_ge(pfull_ready, b + 1)
                    out = begin(key)
                    for qt in range(QT):
                        ins = nc.tensor.transpose(out[0:NTEXT, qt * P:(qt + 1) * P], pfull[:, 1, qt, :], ident[:])
                elif kind == "SEM":
                    taken(pe, ("PT", s))
                    out = begin(key)
                    for qt in range(QT):
                        ins = mm(out[:, qt * T:(qt + 1) * T], pfullT[:, qt * P:(qt + 1) * P], textip[:],
                                 start=True, stop=True)
                elif kind == "SEMT":
                    out = begin(key)
                    for c in range(KT):
                        ins = mm(out[:, c * S:(c + 1) * S], textip[:, c * P:(c + 1) * P], pfullT[:],
                                 start=True, stop=True)
                ins.then_inc(hop_full, 1)

            pe.wait_ge(ones_ready, 1)
            pe.wait_ge(ipsq_ready, 1)
            for e in range(2):
                ins = mm(bank[5][:, 0:B * NIP0], ones[:], ipsq[:, e].rearrange("p b n -> p (b n)"),
                         start=(e == 0), stop=(e == 1))
            ins.then_inc(hop_full, 1)

            for s in range(FIRST, LAST + 1):
                at = hops(s)
                exp, maxi = 0 <= s < SLOTS, 0 <= s + 2 < SLOTS
                for j in range(QUADS):
                    if exp:
                        scores_for_exp(s, 4 * j)
                        scores_for_exp(s, 4 * j + 1)
                    if maxi:
                        scores_for_max(s + 2, j, 0)
                        scores_for_max(s + 2, j, 1)
                    if exp and j:
                        values_product(s, j - 1)
                    if exp:
                        scores_for_exp(s, 4 * j + 2)
                        scores_for_exp(s, 4 * j + 3)
                    if maxi:
                        scores_for_max(s + 2, j, 2)
                        scores_for_max(s + 2, j, 3)
                    if exp and j and layer(s) == 0:
                        if s == 0 and j == 1:
                            pe.wait_ge(text_masked, 1)
                        text_product(s, j - 1)
                    for key in at[j]:
                        hop(key)
                for key in at[5]:
                    hop(key)
                if exp:
                    values_product(s, QUADS - 1)
                    if layer(s) == 0:
                        text_product(s, QUADS - 1)

        @block.scalar
        def _(act):
            def copy(out, in_, scale=None):
                if scale is None:
                    return nc.scalar.activation(out, in_, ACT.Copy)
                return nc.scalar.activation(out, in_, ACT.Copy, scale=scale)

            def exponentials(s, h):
                n = s * H + h
                act.wait_ge(st_full, n + 1)
                if n >= 8 and h % 4 == 0:
                    q = s * QUADS + h // 4
                    act.wait_ge(o_full, q - 1)
                    if q - 1 <= B * QUADS:
                        act.wait_ge(y_full, 4 * (q - 1))
                    elif q - 2 < B * QUADS:
                        act.wait_ge(y_full, B * H)
                nc.scalar.activation(probs[:, h % 8].rearrange("p c q -> p (c q)"), bank[n % 2][:], ACT.Exp,
                                     scale=SCALE).then_inc(probs_ready, 1)

            def take_out(s, j):
                l = layer(s)
                n = s * QUADS + j
                per = 4 * HROWS[l] // P
                if j == 0 and s >= 1:
                    last = t_rounds(layer(s - 1))
                    act.wait_ge(hop_full, full_of(("T", s - 1, len(last) - 1, QT - 1)))
                act.wait_ge(o_full, n + 1)
                copy(outT[:, per * j:per * (j + 1), :],
                     bank[4][:, 0:per * S].rearrange("p (u q) -> p u q", u=per)).then_inc(outT_ready, 1)

            def square_norms(s, j):
                for h in quad_heads(j):
                    n = s * H + h
                    act.wait_ge(y_full, n + 1)
                    for qt in range(QT):
                        y = bank[6 + n % 2][:, qt * E:(qt + 1) * E]
                        ins = nc.scalar.activation(y, y, ACT.Square, accum_out=norm2[:, s % 2, qt, h:h + 1])
                    ins.then_inc(y_free, 1)

            def hop(key):
                kind, s = key[0], key[1]
                l, b = layer(s), batch(s)
                n, hb, _ = plan.hop[key]
                src = bank[hb]
                if kind in ("K", "Q"):
                    act.wait_ge(hop_full, n + 1)
                    dst, stored = (ksplit, k_stored) if kind == "K" else (qsplit, q_stored)
                    if s:
                        act.wait_ge(stored, 16 * s)
                    if l == 1:
                        if kind == "K":
                            if b:
                                act.wait_ge(hop_full, full_of(("FULL", s - 1)))
                            copy(kfull[:], src[0:HALF].rearrange("p (h t) -> p h t", h=2)[:, :, 0:NTEXT])\
                                .then_inc(full_ready, 1)
                        else:
                            copy(qfull[:].rearrange("p h q -> p (h q)"), src[0:HALF]).then_inc(full_ready, 1)
                    copy(dst[:, 0].rearrange("p h t -> p (h t)"), src[0:HALF]).then_inc(high_ready, 1)
                elif kind == "M":
                    act.wait_ge(hop_full, n + 1)
                    if s:
                        act.wait_ge(m_stored, 16 * s)
                    nblk = 3 * len(SEGS[l]) * H // 120
                    copy(maxT[:, 0:nblk].rearrange("p n q -> p (n q)"), src[:].bitcast(BF16)[0:120, 0:nblk * S])\
                        .then_inc(hop_taken[hb], 1)
                elif kind == "T" and l == 0 and key[2:] == (len(t_rounds(0)) - 1, QT - 1):
                    act.wait_ge(norm_ready, s + 1)
                    nc.scalar.activation(nrm[:, 2], nrm[:, 1], ACT.Sqrt).then_inc(root_ready, 1)
                    act.wait_ge(fused_ready, s + 1)
                    nc.scalar.activation(fused[:, 2], fused[:, 1], ACT.Exp, scale=SCALE).then_inc(fexp_ready, 1)
                elif kind == "AT":
                    act.wait_ge(hop_full, n + 1)
                    copy(attnT[:].rearrange("p h q -> p (h q)"), src[0:HALF]).then_inc(hop_taken[hb], 1)
                elif kind == "V":
                    act.wait_ge(hop_full, n + 1)
                    buf = vals[PATTERN[l]]
                    if key[2] == 0:
                        act.wait_ge(vals_zeroed, 3 if l == 3 else 2)
                        if s >= 2:
                            act.wait_ge(o_full, (s - 1) * QUADS)
                    for i, (c, g) in enumerate(v_parts(l)[key[2]]):
                        ins = copy(buf[:, s % 2, c, :, 9 * g:9 * g + D],
                                   src[:, i * C:(i + 1) * C].rearrange("p (h d) -> p h d", h=H),
                                   segmask[:, PATTERN[l], c, g:g + 1])
                    if l == 0:
                        for c in range(KT):
                            ins = copy(buf[:, s % 2, c, :, 9:9 + NIP0],
                                       src[:, 2 * C + c * NIP0:2 * C + (c + 1) * NIP0].unsqueeze(1)
                                       .broadcast_to([P, H, NIP0]), segmask[:, 0, c, 0:1])
                    ins.then_inc(hop_taken[hb], 1)
                elif kind == "VIP":
                    act.wait_ge(hop_full, n + 1)
                    if s >= 2 and key[2] == 0:
                        act.wait_ge(attn_ready, s - 1)
                    m = 3 if key[2] == 0 else 1
                    copy(v_ip[:, s % 2, 3 * key[2]:3 * key[2] + m, :],
                         src[:, 0:m * C].rearrange("p (n c) -> p n c", n=m)).then_inc(hop_taken[hb], 1)
                elif kind == "FULL":
                    act.wait_ge(hop_full, n + 1)
                    if b:
                        act.wait_ge(hop_full, full_of(("SEMT", s - 1)))
                    copy(textip[:, NTEXT:T], src[0:NTEXT, 0:T - NTEXT]).then_inc(textip_ready, 1)
                    act.wait_ge(bias_ready, b + 1)
                    for qt in range(QT):
                        ins = nc.scalar.activation(pfull[:, 0, qt, :], src[:, 256 + qt * NTEXT:256 + (qt + 1) * NTEXT],
                                                   ACT.Exp, bias=fstat[:, 1, qt:qt + 1], scale=SCALE,
                                                   accum_out=fstat[:, 2, qt:qt + 1])
                    ins.then_inc(hop_taken[hb], 1)
                elif kind == "PT":
                    act.wait_ge(hop_full, n + 1)
                    copy(pfullT[:], src[0:NTEXT, 0:S]).then_inc(hop_taken[hb], 1)
                elif kind in ("SEM", "SEMT"):
                    act.wait_ge(hop_full, n + 1)
                    if kind == "SEM" and b:
                        act.wait_ge(s_full, s * 4 * QUADS)
                    if kind == "SEMT" and b == 3:
                        act.wait_ge(st_full, st_count(s - 3, H - 1))
                    copy(semq[:, 0] if kind == "SEM" else semk[:, s % 3, 0], src[:], 0.5).then_inc(high_ready, 1)

            act.wait_ge(loaded_const, 16 * 8)
            act.wait_ge(hop_taken[5], 1)
            nc.scalar.activation(ipn[:, 1], ipn[:, 0], ACT.Sqrt).then_inc(root_ready, 1)
            for s in range(FIRST, LAST + 1):
                at = hops(s)
                exp = 0 <= s < SLOTS
                for j in range(QUADS):
                    if exp:
                        exponentials(s, 4 * j)
                        exponentials(s, 4 * j + 1)
                        if j:
                            take_out(s, j - 1)
                        exponentials(s, 4 * j + 2)
                        exponentials(s, 4 * j + 3)
                        if j and layer(s) == 0:
                            if j == 1 and s >= 2:
                                act.wait_ge(attn_ready, s - 1)
                            square_norms(s, j - 1)
                    for key in at[j]:
                        hop(key)
                for key in at[5]:
                    hop(key)
                if exp:
                    take_out(s, QUADS - 1)
                    if layer(s) == 0:
                        square_norms(s, QUADS - 1)

        @block.vector
        def _(dve):
            steps = [0]

            def link(ins):
                steps[0] += 1
                ins.then_inc(dve_step, 1)
                dve.wait_ge(dve_step, steps[0])

            tt, ts, stt = nc.vector.tensor_tensor, nc.vector.tensor_scalar, nc.vector.scalar_tensor_tensor

            def maxima(a, j, u):
                qt, half = heads_of(u)
                n, b, _ = plan.unit[(a, j, u)]
                l = layer(a)
                if j == 0 and u == 0 and a >= 2:
                    dve.wait_ge(maxsplit_ready, a - 1)
                dve.wait_ge(s_full, n + 1)
                src = bank[b][:].rearrange("p (s t) -> p s t", s=2)
                dst = negmax[:, a % 2, qt, 0:len(SEGS[l]) * H]\
                    .rearrange("p (g e s) -> p s g e", g=len(SEGS[l]), e=2)[:, 2 * j:2 * j + 2, :, half]

                def take(g, z):
                    lo, hi = SEGS[l][g][0], SEGS[l][z - 1][1]
                    return nc.vector.tensor_reduce(
                        dst[:, :, g:z], src[:, :, lo:hi].rearrange("p s (g k) -> p s g k", g=z - g),
                        AX.X, ALU.max, negate=True)
                if l == 0:
                    nc.vector.tensor_copy(
                        s_ip[:, batch(a), qt].rearrange("p (s e) n -> p s e n", e=2)[:, 2 * j:2 * j + 2, half, :],
                        src[:, :, T - NIP0:T])
                runs = [(0, 1), (1, 3), (3, 4)] if l == 3 else [(0, 1), (1, 2)]
                for g, z in runs:
                    ins = take(g, z)
                ins.then_inc(s_free, 1)

            def image_keys(s):
                b = batch(s)
                dve.wait_ge(y_free, (s + 1) * H)
                link(tt(nrm[:, 0], norm2[:, s % 2], rsum[:, :, :, 0], ALU.mult))
                link(tt(nrm[:, 3], nrm[:, 0], rsum[:, :, :, 0], ALU.mult))
                nc.vector.tensor_scalar_max(nrm[:, 1], nrm[:, 3], EPS2).then_inc(norm_ready, 1)
                dve.wait_ge(root_ready, s + 2)
                link(nc.vector.reciprocal(fsum[:, 0], nrm[:, 2]))
                link(tt(fused[:, 0], dots[:], fsum[:, 0].unsqueeze(3).broadcast_to([P, QT, H, NIP0]), ALU.mult))
                link(tt(fused[:, 1].rearrange("p q h n -> p (q h) n"), fused[:, 0].rearrange("p q h n -> p (q h) n"),
                        ipn[:, 2, b].unsqueeze(1).broadcast_to([P, QT * H, NIP0]), ALU.mult))
                link(stt(fused[:, 0].rearrange("p q h n -> p (q h n)"), fused[:, 1].rearrange("p q h n -> p (q h n)"),
                         0.5 / SCALE, s_ip[:, b].rearrange("p q h n -> p (q h n)"), ALU.mult, ALU.add))
                link(nc.vector.tensor_reduce(fsum[:, 1], fused[:, 0], AX.X, ALU.max))
                tt(fused[:, 1], fused[:, 0], fsum[:, 1].unsqueeze(3).broadcast_to([P, QT, H, NIP0]), ALU.subtract)\
                    .then_inc(fused_ready, 1)
                dve.wait_ge(fexp_ready, s + 1)
                link(nc.vector.tensor_reduce(fsum[:, 2], fused[:, 2], AX.X, ALU.add))
                link(nc.vector.reciprocal(fsum[:, 3], fsum[:, 2]))
                link(tt(fsum[:, 4], fsum[:, 3], spatial[:].unsqueeze(2).broadcast_to([P, QT, H]), ALU.mult))
                link(tt(fused[:, 0], fused[:, 2], fsum[:, 4].unsqueeze(3).broadcast_to([P, QT, H, NIP0]), ALU.mult))
                taken(dve, ("VIP", s, 1))
                for qt in range(QT):
                    for n in range(NIP0):
                        ins = tt(ipprod[:, n].rearrange("p (h d) -> p h d", h=H),
                                 v_ip[:, s % 2, n].rearrange("p (h d) -> p h d", h=H),
                                 fused[:, 0, qt, :, n].unsqueeze(2).broadcast_to([P, H, D]), ALU.mult)
                    link(ins)
                    link(nc.vector.tensor_reduce(ipout[:], ipprod[:].rearrange("p n c -> p c n"), AX.X, ALU.add))
                    ins = tt(attn[:, qt], ipout[:], attn[:, qt], ALU.add)
                    if qt < QT - 1:
                        link(ins)
                ins.then_inc(attn_ready, 1)

            def hop(key):
                kind, s = key[0], key[1]
                l, b = layer(s), batch(s)
                n, hb, before = plan.hop[key]
                src = bank[hb]
                if kind in ("K", "Q", "SEM", "SEMT"):
                    i = plan.split[key]
                    dve.wait_ge(high_ready, i + 1)
                    if i:
                        dve.wait_ge(split_ready, i)
                    if kind in ("K", "Q"):
                        high = (ksplit if kind == "K" else qsplit)[:, 0].rearrange("p h t -> p (h t)")
                        ins = tt(rest[0:HALF, 0], src[0:HALF], high, ALU.subtract)
                    else:
                        high = semq[:, 0] if kind == "SEM" else semk[:, s % 3, 0]
                        ins = stt(rest[:, 0], src[:], 0.5, high, ALU.mult, ALU.subtract)
                    ins.then_inc(hop_taken[hb], 1)
                elif kind == "T":
                    _, _, rnd, qt = key
                    dve.wait_ge(hop_full, n + 1)
                    units = t_rounds(l)[rnd]
                    per = P // HROWS[l]
                    h0, h1 = units[0] * per, (units[-1] + 1) * per
                    nh, g = h1 - h0, 1 if l == 0 else len(SEGS[l])
                    view = tr_view(l, key, units)
                    if rnd == 0 and qt == 0 and s:
                        dve.wait_ge(hop_full, full_of(("AT", s - 1)))
                    if l == 0:
                        link(nc.vector.reciprocal(rsum[:, qt, h0:h1, 0], view[:, :, D]))
                        tt(attn[:, qt, h0 * D:h1 * D].rearrange("p (h d) -> p h d", h=nh), view[:, :, 0:D],
                           rsum[:, qt, h0:h1, 0:1].broadcast_to([P, nh, D]), ALU.mult)
                        tt(dots[:, qt, h0:h1], view[:, :, 9:9 + NIP0],
                           rsum[:, qt, h0:h1, 0:1].broadcast_to([P, nh, NIP0]), ALU.mult).then_inc(hop_taken[hb], 1)
                        if (rnd, qt) == (len(t_rounds(0)) - 1, QT - 1):
                            taken(dve, key)
                            image_keys(s)
                    else:
                        parts = view[:, :, 0:9 * g].rearrange("p h (g k) -> p h g k", k=9)
                        link(nc.vector.reciprocal(rsum[:, qt, h0:h1, 0:g], parts[:, :, :, D]))
                        if l == 1:
                            link(ts(rsum[:, qt, h0:h1, 1], rsum[:, qt, h0:h1, 1], spatial[:, qt:qt + 1], None, ALU.mult))
                        tt(scaled[:, 0:nh, 0:g], parts[:, :, :, 0:D],
                           rsum[:, qt, h0:h1, 0:g].unsqueeze(3).broadcast_to([P, nh, g, D]), ALU.mult)\
                            .then_inc(hop_taken[hb], 1)
                        taken(dve, key)
                        ins = nc.vector.tensor_reduce(attn[:, qt, h0 * D:h1 * D].rearrange("p (h d) -> p h d", h=nh),
                                                      scaled[:, 0:nh, 0:g].rearrange("p h g d -> p h d g"),
                                                      AX.X, ALU.add)
                        if (rnd, qt) == (len(t_rounds(l)) - 1, QT - 1):
                            ins.then_inc(attn_ready, 1)
                        else:
                            link(ins)
                elif kind == "OUT":
                    dve.wait_ge(hop_full, n + 1)
                    for half in range(2):
                        x = xT[:, half, b * S:(b + 1) * S]
                        ins = stt(x, src[0:HALF, half * S:(half + 1) * S], bo[:, l, half:half + 1], x, ALU.add, ALU.add)
                    ins.then_inc(hop_taken[hb], 1)
                elif kind == "FULL":
                    dve.wait_ge(textip_ready, b + 1)
                    link(nc.vector.tensor_reduce(fstat[:, 0], src[:, 256:256 + QT * NTEXT]
                                                 .rearrange("p (q t) -> p q t", q=QT), AX.X, ALU.max, negate=True))
                    ts(fstat[:, 1], fstat[:, 0], SCALE, None, ALU.mult).then_inc(bias_ready, 1)
                    taken(dve, key)
                    link(nc.vector.reciprocal(fstat[:, 3], fstat[:, 2]))
                    for qt in range(QT):
                        ins = ts(pfull[:, 1, qt], pfull[:, 0, qt], fstat[:, 3, qt:qt + 1], None, ALU.mult)
                    ins.then_inc(pfull_ready, 1)

            dve.wait_ge(loaded_ctx, 16)
            ip = ctxT[:].rearrange("p e (b t) -> p e b t", b=B)[:, :, :, T - NIP0:T]
            for e in range(2):
                ins = tt(ipsq[:, e], ip[:, e], ip[:, e], ALU.mult)
            ins.then_inc(ipsq_ready, 1)
            dve.wait_ge(hop_full, 1)
            nc.vector.tensor_scalar_max(ipn[:, 0].rearrange("p b n -> p (b n)"), bank[5][:, 0:B * NIP0], EPS2)\
                .then_inc(hop_taken[5], 1)
            dve.wait_ge(root_ready, 1)
            link(nc.vector.reciprocal(ipn[:, 2], ipn[:, 1]))
            dve.wait_ge(loaded_const, 16 * 8)
            odd = text[:].rearrange("p (b c) e -> p c b e", c=KT)[:, 1]
            ts(odd, odd, segmask[:, 0, 1, 0:1], None, ALU.mult).then_inc(text_masked, 1)
            dve.wait_ge(ones_ready, 1)

            def mark_segments(zeroed, patterns):
                dve.wait_ge(vals_zeroed, zeroed)
                for pattern, segs in patterns:
                    for c in range(KT):
                        for g in range(segs):
                            ins = ts(vals[pattern][:, :, c, :, 9 * g + D],
                                     ones[:, 0:2 * H].rearrange("p (i h) -> p i h", i=2),
                                     segmask[:, pattern, c, g:g + 1], None, ALU.mult)
                ins.then_inc(vals_marked, 1)

            mark_segments(2, ((0, 1), (1, 2)))
            for s in range(FIRST, LAST + 1):
                at = hops(s)
                maxi = 0 <= s + 2 < SLOTS
                for j in range(QUADS):
                    if maxi:
                        for u in range(4):
                            maxima(s + 2, j, u)
                    for key in at[j]:
                        hop(key)
                for key in at[5]:
                    hop(key)
                if s == 7:
                    mark_segments(3, ((2, 4),))

        @block.gpsimd
        def _(pool):
            steps = [0]

            def link(ins):
                steps[0] += 1
                ins.then_inc(pool_step, 1)
                pool.wait_ge(pool_step, steps[0])

            nc.gpsimd.memset(ones[:], 1.0).then_inc(ones_ready, 1)
            for v in (vals_wide, vals_mid):
                nc.gpsimd.memset(v[:], 0.0).then_inc(vals_zeroed, 1)
            nc.gpsimd.memset(textip[:, 0:NTEXT], 0.0).then_inc(ones_ready, 1)

            def lower_parts(key):
                kind, s = key[0], key[1]
                i = plan.split[key]
                taken(pool, key)
                if kind in ("K", "Q"):
                    dst = [(ksplit if kind == "K" else qsplit)[:, p].rearrange("p h t -> p (h t)") for p in (1, 2)]
                    src = rest[0:HALF, 0]
                else:
                    buf = semq[:] if kind == "SEM" else semk[:, s % 3]
                    dst, src = [buf[:, 1], buf[:, 2]], rest[:, 0]
                link(nc.gpsimd.tensor_copy(dst[0], src))
                nc.gpsimd.tensor_tensor(dst[1], src, dst[0], ALU.subtract).then_inc(split_ready, 1)

            def split_maxima(a):
                n = len(SEGS[layer(a)]) * H
                pool.wait_ge(s_free, (a + 1) * 4 * QUADS)
                if a:
                    pool.wait_ge(hop_full, full_of(("M", a - 1)))
                src, left = negmax[:, a % 2, :, 0:n], maxrest[:, :, 0:n]
                flat = maxsplit[:].rearrange("p q a n -> p q (a n)")
                part = [flat[:, :, p * n:(p + 1) * n] for p in range(3)]
                link(nc.gpsimd.tensor_copy(part[0], src))
                link(nc.gpsimd.tensor_tensor(left, src, part[0], ALU.subtract))
                link(nc.gpsimd.tensor_copy(part[1], left))
                nc.gpsimd.tensor_tensor(part[2], left, part[1], ALU.subtract).then_inc(maxsplit_ready, 1)

            for s in range(FIRST, LAST + 1):
                at = hops(s)
                for j in range(QUADS):
                    for key in at[j]:
                        if key[0] in ("K", "Q"):
                            lower_parts(key)
                if 0 <= s + 2 < SLOTS:
                    split_maxima(s + 2)
                for key in at[5]:
                    if key[0] in ("SEM", "SEMT"):
                        lower_parts(key)
                if s == 6:
                    pool.wait_ge(o_full, B * QUADS)
                    nc.gpsimd.memset(vals_wide[:], 0.0).then_inc(vals_zeroed, 1)


def kernel(**inputs):
    import ml_dtypes
    import numpy as np
    import concourse.bacc as bacc
    from concourse.bass_utils import run_bass_kernel_spmd as run

    f = lambda name: np.asarray(inputs[name])

    def by_half(w):
        return w.reshape(w.shape[0], NS, 2, D).transpose(0, 2, 3, 1).reshape(w.shape[0], C)

    def rows(w):
        n = HALF if w.shape[0] == C else P
        return w.reshape(-1, n, w.shape[1]).transpose(1, 0, 2)

    names = [
        dict(q="L0_xattn_W_q", k=["L0_xattn_W_k", "L0_xattn_W_k_ip"], v=["L0_xattn_W_v", "L0_xattn_W_v_ip"],
             o="L0_xattn_W_out", b="L0_xattn_b_out"),
        dict(q="L1_xattn_Wq", k=["L1_xattn_Wk", "L1_xattn_Wk_ip"], v=["L1_xattn_Wv", "L1_xattn_Wv_ip"],
             o="L1_xattn_Wout", b="L1_xattn_bout"),
        dict(q="L2_xattn_Wq", k=["L2_xattn_Wk", "L2_xattn_Wk_ip"], v=["L2_xattn_Wv", "L2_xattn_Wv_ip"],
             o="L2_xattn_Wo", b="L2_xattn_bo"),
        dict(q="L3_xattn_to_q_w", k=[f"L3_xattn_to_k_{x}w" for x in ("", "object_", "others_", "ip_")],
             v=[f"L3_xattn_to_v_{x}w" for x in ("", "object_", "others_", "ip_")],
             o="L3_xattn_to_out_w", b="L3_xattn_to_out_b"),
    ]
    w = lambda l, name: f(name).T if l == 2 else f(name)
    arrays = {
        "xT": f("x").reshape(B * S, 2, HALF).transpose(2, 1, 0),
        "ctxT": f("ctx_2048").reshape(B * T, 2, P).transpose(2, 1, 0),
        "text": f("ctx_2048").reshape(B * KT, P, E).transpose(1, 0, 2),
        "spatial": f("fside_S_0").reshape(QT, P).T,
        "wq": np.stack([rows(by_half(w(l, n["q"]))) for l, n in enumerate(names)], 1),
        "wo": np.stack([rows(w(l, n["o"])) for l, n in enumerate(names)], 1),
        "bo": np.stack([f(n["b"]).reshape(2, HALF).T for n in names], 1),
    }
    for l, n in enumerate(names):
        arrays[f"wk{l}"] = np.stack([rows(by_half(w(l, x))) for x in n["k"]], 1)
        arrays[f"wv{l}"] = np.stack([rows(w(l, x)) for x in n["v"]], 1)
    masks = np.zeros((P, 3, KT, 4), np.float32)
    for l in (0, 1, 3):
        marks = np.zeros((len(SEGS[l]), T), np.float32)
        for g, (a, z) in enumerate(SEGS[l]):
            marks[g, a:z] = 1
            masks[:, PATTERN[l], :, g] = marks[g].reshape(KT, P).T
        arrays[f"marks{PATTERN[l]}"] = np.tile(marks, (3, NS)).astype(ml_dtypes.bfloat16)
    arrays["segmask"] = masks
    arrays["ident"] = np.eye(P, dtype=np.float32)
    arrays["identb"] = np.eye(P, dtype=np.float32).astype(ml_dtypes.bfloat16)

    nc = bacc.Bacc("TRN2", target_bir_lowering=False, num_devices=1)
    arrays = {f"in_{k}": np.ascontiguousarray(a) for k, a in arrays.items()}
    t = {k[3:]: nc.dram_tensor(k, a.shape, mybir.dt.from_np(a.dtype), kind="ExternalInput").ap()
         for k, a in arrays.items()}
    t["out"] = nc.dram_tensor("out", (HALF, 2, B * S), F32, kind="ExternalOutput").ap()
    program(nc, t)
    r = run(nc, [arrays], core_ids=[0])
    return r.results[0]["out"].transpose(2, 1, 0).reshape(B, S, C)
```

```python
from contextlib import ExitStack

import concourse.bass as bass
from concourse import mybir

F32 = mybir.dt.float32
BF16 = mybir.dt.bfloat16
ACT = mybir.ActivationFunctionType
ALU = mybir.AluOpType
AX = mybir.AxisListType

P = 128
B, S, C, E, T = 4, 256, 160, 256, 256
H, D = 20, 8
NL = 4
SLOTS = NL * B
SCALE = float(D) ** -0.5
HALF = C // 2
QUADS = H // 4
NS = H // 2
NPROD = 6
ROWS = NPROD * D
QT = S // P
KT = T // P
EPS2 = 1e-24

SEGS = [
    [(0, 252), (252, 256)],
    [(0, 77), (77, 256)],
    [(0, 77), (77, 256)],
    [(0, 77), (77, 81), (81, 85), (85, 256)],
]
NTEXT = 77
PATTERN = [0, 1, 1, 2]
HROWS = [32, 32, 32, 64]
NIP0 = 4


def layer(s):
    return s // B


def batch(s):
    return s % B


def v_parts(l):
    segs = SEGS[l][:1] if l == 0 else SEGS[l]
    pairs = [(c, g) for c in range(KT) for g, (a, z) in enumerate(segs) if a < (c + 1) * P and z > c * P]
    return [pairs[i:i + 3] for i in range(0, len(pairs), 3)]


def t_rounds(l):
    units = H * HROWS[l] // P
    n = 3 if l < 3 else 4
    return [list(range(i, min(i + n, units))) for i in range(0, units, n)]


def score_quad(s, j):
    g = s * QUADS + j - 2
    return g // QUADS + 2, g % QUADS


MID, END = 0, 1
TAIL = 2 * QUADS


def hops(s):
    at = [[] for _ in range(2 * QUADS + 1)]
    ahead, following, now, last = [x if 0 <= x < SLOTS else None for x in (s + 3, s + 1, s, s - 1)]
    if ahead is not None:
        at[0].append(("K", ahead))
    if s == -1:
        at[0].append(("NORM", 0))
    if s + 2 in range(B, 2 * B):
        at[0].append(("SEM", s + 2))
        at[1].append(("SEMT", s + 2))
    if last is not None:
        late = [("T", last, n, qt) for n in range(1, len(t_rounds(layer(last)))) for qt in range(QT)]
        if len(late) == 2:
            at[1].append(late[0])
            at[2].append(late[1])
        else:
            at[0].append(late[0])
            at[1].append(late[1])
            at[2] += late[2:]
        at[5 if layer(last) == 0 else 4].append(("AT", last))
        at[6].append(("OUT", last))
    if following is not None:
        rounds = [("V", following, n) for n in range(len(v_parts(layer(following))))]
        at[3].append(rounds[0])
        at[5].append(("M", following))
        at[7] += rounds[1:]
        if layer(following) == 0:
            at[7].append(("VIP", following, 0))
            at[9].append(("VIP", following, 1))
    if ahead is not None:
        at[8].append(("Q", ahead))
    if now is not None:
        at[8].append(("T", now, 0, 0))
        at[9].append(("T", now, 0, 1))
    if ahead is not None and layer(ahead) == 1:
        at[9].append(("FULL", ahead))
        at[TAIL].append(("PT", ahead))
    return at


FIRST, LAST = -3, SLOTS


def hop_banks(s):
    return [5] if 0 <= s < B else [5, 6]


def score_banks(s):
    return [2, 3] if s < B else [2, 3, 7]


class Plan:

    def __init__(self):
        self.hop, n, used = {}, 0, {5: 0, 6: 0}
        for s in range(FIRST, LAST + 1):
            for pos in hops(s):
                for key in pos:
                    bank = hop_banks(s)[n % len(hop_banks(s))]
                    self.hop[key] = (n, bank, used[bank])
                    used[bank] += 1
                    n += 1
        on6 = [(n, k, used) for k, (n, bank, used) in self.hop.items() if bank == 6]
        start = self.hop[("K", 3)][0]
        self.hops_on_6_before_text = sum(1 for n, _, _ in on6 if n < start)
        self.first_on_6_after_text = min((n, k) for n, k, _ in on6 if n > start)[1]
        self.unit, last, n = {}, {}, 0
        for a in range(SLOTS):
            for j in range(QUADS):
                for u in range(4):
                    banks = score_banks(a - 2 + (j + 2) // QUADS)
                    bank = banks[n % len(banks)]
                    self.unit[(a, j, u)] = (n, bank, last.get(bank))
                    last[bank] = n
                    n += 1
        self.split, n = {}, 0
        for s in range(FIRST, LAST + 1):
            for pos in hops(s):
                for key in pos:
                    if key[0] in ("K", "Q", "SEMT"):
                        self.split[key] = n
                        n += 1


def program(nc, t):
    plan = Plan()
    with ExitStack() as ctx:
        def sb(name, shape, dt=F32):
            return ctx.enter_context(nc.sbuf_tensor(name, shape, dt))

        def sem(name):
            return ctx.enter_context(nc.semaphore(name))

        bank = [ctx.enter_context(nc.psum_tensor(f"bank{i}", [P, 512], F32)) for i in range(8)]

        xT = sb("xT", [HALF, 2, B * S])
        ctxT = sb("ctxT", [P, 2, B * T])
        text = sb("text", [P, B * KT, E])
        wq = sb("wq", [HALF, NL, 2, C])
        wo = sb("wo", [HALF, NL, 2, C])
        bo = sb("bo", [HALF, NL, 2])
        wk = [sb(f"wk{l}", [P, len(SEGS[l]), 2, C]) for l in range(NL)]
        wv = [sb(f"wv{l}", [P, len(SEGS[l]), 2, C]) for l in range(NL)]
        spatial = sb("spatial", [P, QT])
        segmask = sb("segmask", [P, 3, KT, 4])
        ident = sb("ident", [P, P])
        identb = sb("identb", [P, P], BF16)
        ones = sb("ones", [P, P])
        kstack = sb("kstack", [P, 4, NS, T], BF16)
        qstack = sb("qstack", [P, 4, NS, S], BF16)
        ksplit = sb("ksplit", [HALF, 3, 2, T], BF16)
        qsplit = sb("qsplit", [HALF, 3, 2, S], BF16)
        rest = sb("rest", [P, 1, 512])
        negmax = sb("negmax", [P, 2, QT, 4 * H])
        maxrest = sb("maxrest", [P, QT, 4 * H])
        maxsplit = sb("maxsplit", [P, QT, 3, 4 * H], BF16)
        maxT = sb("maxT", [120, 2, S], BF16)
        probs = sb("probs", [P, 8, KT, S])
        vals_wide = sb("vals_wide", [P, 2, KT, H, 64])
        vals_mid = sb("vals_mid", [P, 2, KT, H, 32])
        vals = [vals_wide[:, :, :, :, 0:32], vals_mid[:], vals_wide[:]]
        outT = sb("outT", [P, H // 2, S])
        rsum = sb("rsum", [P, QT, H, 4])
        scaled = sb("scaled", [P, 12, 4, D])
        attn = sb("attn", [P, QT, C])
        attnT = sb("attnT", [HALF, 2, S])
        s_ip = sb("s_ip", [P, 4, QT, H, NIP0])
        norm2 = sb("norm2", [P, 2, QT, H])
        dots = sb("dots", [P, QT, H, NIP0])
        ipsq = sb("ipsq", [P, 2, B, NIP0])
        ipn = sb("ipn", [P, 3, B, NIP0])
        v_ip = sb("v_ip", [P, 2, NIP0, C])
        nrm = sb("nrm", [P, 4, QT, H])
        fused = sb("fused", [P, 3, QT, H, NIP0])
        fsum = sb("fsum", [P, 5, QT, H])
        ipprod = sb("ipprod", [P, NIP0, C])
        ipout = sb("ipout", [P, C])
        qfull = sb("qfull", [HALF, 2, S])
        kfull = sb("kfull", [HALF, 2, NTEXT])
        textip = sb("textip", [NTEXT, T])
        pfull = sb("pfull", [P, 2, QT, NTEXT])
        fstat = sb("fstat", [P, 4, QT])
        pfullT = sb("pfullT", [NTEXT, S])
        semq = sb("semq", [P, 2, QT * T])
        semk = sb("semk", [P, 3, 3, KT * S], BF16)

        k_dram = nc.dram_tensor("k_dram", [SLOTS, 3, 2, HALF * T], BF16).ap()
        q_dram = nc.dram_tensor("q_dram", [SLOTS, 3, 2, HALF * S], BF16).ap()
        m_dram = nc.dram_tensor("m_dram", [SLOTS, 240, S], BF16).ap()

        loaded_x = sem("loaded_x")
        loaded_ctx = [sem(f"loaded_ctx{b}") for b in range(B)]
        loaded_text = sem("loaded_text")
        loaded_wk = [sem(f"loaded_wk{l}") for l in range(NL)]
        loaded_w = [sem(f"loaded_w{l}") for l in range(NL)]
        loaded_const = sem("loaded_const")
        k_stored = sem("k_stored")
        q_stored = sem("q_stored")
        m_stored = sem("m_stored")
        k_loaded = [sem(f"k_loaded{i}") for i in range(4)]
        q_loaded = [sem(f"q_loaded{i}") for i in range(4)]
        m_loaded = [sem(f"m_loaded{i}") for i in range(4)]
        out_stored = sem("out_stored")
        st_full = sem("st_full")
        probs_ready = sem("probs_ready")
        s_full = sem("s_full")
        s_free = sem("s_free")
        o_full = sem("o_full")
        outT_ready = sem("outT_ready")
        y_full = sem("y_full")
        y_free = sem("y_free")
        hop_full = sem("hop_full")
        hop_taken = {5: sem("hop5_taken"), 6: sem("hop6_taken")}
        high_ready = sem("high_ready")
        rest_ready = sem("rest_ready")
        split_ready = sem("split_ready")
        maxsplit_ready = sem("maxsplit_ready")
        attn_ready = sem("attn_ready")
        full_ready = sem("full_ready")
        textip_ready = sem("textip_ready")
        bias_ready = sem("bias_ready")
        pfull_ready = sem("pfull_ready")
        norm_ready = sem("norm_ready")
        root_ready = sem("root_ready")
        fused_ready = sem("fused_ready")
        fexp_ready = sem("fexp_ready")
        text_masked = sem("text_masked")
        ipsq_ready = sem("ipsq_ready")
        vals_zeroed = sem("vals_zeroed")
        vals_marked = sem("vals_marked")
        ones_ready = sem("ones_ready")
        dve_step = sem("dve_step")
        pool_step = sem("pool_step")
        block = ctx.enter_context(nc.Block())

        def heads_of(unit):
            return unit // 2, unit % 2

        def full_of(key):
            return plan.hop[key][0] + 1

        def hop_view(key):
            return bank[plan.hop[key][1]]

        def tr_view(l, key, units):
            r = HROWS[l]
            return hop_view(key)[:, 0:len(units) * P].rearrange("p (h r) -> p h r", r=r)

        def taken(eng, key):
            _, b, before = plan.hop[key]
            eng.wait_ge(hop_taken[b], before + 1)

        def last_values_hop(s):
            return ("V", s, len(v_parts(layer(s))) - 1)

        def st_count(s, h):
            return s * H + h + 1

        def quad_heads(j):
            return range(4 * j, 4 * j + 4)

        def k_dmas(s):
            return 8 if s < B or PATTERN[layer(s)] != PATTERN[layer(s) - 1] else 6

        def k_loaded_count(s):
            return 16 * sum(k_dmas(x) for x in range(batch(s), s + 1, B))

        @block.sync
        def _(sp):
            def load(dst, name, done):
                sp.dma_start(dst, t[name]).then_inc(done, 16)

            load(wk[0][:], "wk0", loaded_wk[0])
            sp.dma_start(ctxT[:, :, 0:T], t["ctxT"][:, :, 0:T]).then_inc(loaded_ctx[0], 16)
            load(wq[:], "wq", loaded_x)
            load(xT[:], "xT", loaded_x)

            def load_later(s):
                if s == FIRST:
                    for b in range(1, B):
                        sp.dma_start(ctxT[:, :, b * T:(b + 1) * T], t["ctxT"][:, :, b * T:(b + 1) * T])\
                            .then_inc(loaded_ctx[b], 16)
                if s == FIRST + 1:
                    for name, dst in (("segmask", segmask), ("ident", ident), ("identb", identb),
                                      ("spatial", spatial), ("wo", wo), ("bo", bo)):
                        load(dst[:], name, loaded_const)
                    load(wv[0][:], "wv0", loaded_w[0])
                    load(text[:], "text", loaded_text)
                if 0 <= s < NL - 1:
                    load(wk[s + 1][:], f"wk{s + 1}", loaded_wk[s + 1])
                    load(wv[s + 1][:], f"wv{s + 1}", loaded_w[s + 1])

            def stack(dst, src, order, done):
                for half in range(2):
                    for row, n, part, step in order:
                        a = src[part:part + (n if step else 1), half, :].rearrange("r (d x) -> r d x", d=D)
                        if not step and n > 1:
                            a = a.broadcast_to([n, D, NS * T])
                        sp.dma_start(dst[64 * half + row * D:64 * half + (row + n) * D, :], a).then_inc(done, 16)

            for s in range(FIRST, LAST):
                load_later(s)
                k = s + 3
                if k < SLOTS:
                    if k >= B:
                        sp.wait_ge(st_full, st_count(k - B, H - 1))
                    sp.wait_ge(split_ready, plan.split[("K", k)] + 1)
                    sp.dma_start(k_dram[k].rearrange("a h (p t) -> p (a h) t", p=HALF),
                                 ksplit[:].rearrange("p a h t -> p (a h) t")).then_inc(k_stored, 16)
                if k < SLOTS:
                    if k_dmas(k) == 8:
                        n = 3 * len(SEGS[layer(k)])
                        for half in range(2):
                            sp.dma_start(kstack[64 * half + ROWS:64 * half + ROWS + n, batch(k)]
                                         .rearrange("r s t -> r (s t)"),
                                         t[f"marks{PATTERN[layer(k)]}"]).then_inc(k_loaded[batch(k)], 16)
                    sp.wait_ge(k_stored, 16 * (k + 1))
                    stack(kstack[:, batch(k)].rearrange("r s t -> r (s t)"), k_dram[k],
                          ((0, 3, 0, 1), (3, 2, 0, 1), (5, 1, 0, 0)), k_loaded[batch(k)])
                if 0 <= s + 1 < SLOTS:
                    m = s + 1
                    nblk = len(SEGS[layer(m)]) * 3 * H // 120
                    taken(sp, ("M", m))
                    sp.dma_start(m_dram[m, 0:nblk * 120].rearrange("(n p) q -> p n q", n=nblk),
                                 maxT[:, 0:nblk, :]).then_inc(m_stored, 16)
                    sp.wait_ge(m_stored, 16 * (m + 1))
                    n = 3 * len(SEGS[layer(m)])
                    for half in range(2):
                        sp.dma_start(qstack[64 * half + ROWS:64 * half + ROWS + n, batch(m)],
                                     m_dram[m, 0:n * H].rearrange("(r h s) q -> h r s q", h=2, s=NS)[half])\
                            .then_inc(m_loaded[batch(m)], 16)
                if s >= 1 and layer(s - 1) == NL - 1:
                    taken(sp, ("OUT", s - 1))
                    b = batch(s - 1)
                    sp.dma_start(t["out"][:, :, b * S:(b + 1) * S], xT[:, :, b * S:(b + 1) * S]).then_inc(out_stored, 16)
                if k < SLOTS:
                    sp.wait_ge(split_ready, plan.split[("Q", k)] + 1)
                    sp.dma_start(q_dram[k].rearrange("a h (p t) -> p (a h) t", p=HALF),
                                 qsplit[:].rearrange("p a h t -> p (a h) t")).then_inc(q_stored, 16)
                    sp.wait_ge(q_stored, 16 * (k + 1))
                    stack(qstack[:, batch(k)].rearrange("r s t -> r (s t)"), q_dram[k],
                          ((0, 3, 0, 0), (3, 2, 1, 0), (5, 1, 2, 0)), q_loaded[batch(k)])
            taken(sp, ("OUT", SLOTS - 1))
            b = B - 1
            sp.dma_start(t["out"][:, :, b * S:(b + 1) * S], xT[:, :, b * S:(b + 1) * S]).then_inc(out_stored, 16)
            sp.wait_ge(out_stored, 16 * B)

        @block.tensor
        def _(pe):
            mm = nc.tensor.matmul

            def begin(key):
                n, b, before = plan.hop[key]
                if before:
                    pe.wait_ge(hop_taken[b], before)
                if key == plan.first_on_6_after_text:
                    pe.wait_ge(y_free, B * H)
                return bank[b]

            def scores_for_max(a, j, u):
                qt, half = heads_of(u)
                n, b, last = plan.unit[(a, j, u)]
                if j == 0 and u == 0:
                    pe.wait_ge(k_loaded[batch(a)], k_loaded_count(a))
                    pe.wait_ge(q_loaded[batch(a)], 96 * (layer(a) + 1))
                if last is not None:
                    pe.wait_ge(s_free, last + 1)
                elif b == 7:
                    pe.wait_ge(y_free, B * H)
                r0 = 64 * half
                out = bank[b]
                for i in range(2):
                    ins = mm(out[:, i * T:(i + 1) * T],
                             qstack[r0:r0 + ROWS, batch(a), 2 * j + i, qt * P:(qt + 1) * P],
                             kstack[r0:r0 + ROWS, batch(a), 2 * j + i, :],
                             start=True, stop=True)
                ins.then_inc(s_full, 1)

            def scores_for_exp(s, h):
                if h == 0:
                    pe.wait_ge(m_loaded[batch(s)], 32 * (layer(s) + 1))
                n = s * H + h
                if n >= 2:
                    pe.wait_ge(probs_ready, n - 1)
                r0, rows = 64 * (h % 2), ROWS + 3 * len(SEGS[layer(s)])
                out = bank[n % 2]
                sem_add = layer(s) == 1
                if sem_add:
                    if h == 0:
                        pe.wait_ge(split_ready, plan.split[("SEMT", s)] + 1)
                    for part in range(3):
                        mm(out[:], identb[:], semk[:, s % 3, part, :], start=(part == 0), stop=False)
                for c in range(KT):
                    ins = mm(out[:, c * S:(c + 1) * S],
                             kstack[r0:r0 + rows, batch(s), h // 2, c * P:(c + 1) * P],
                             qstack[r0:r0 + rows, batch(s), h // 2, :],
                             start=not sem_add, stop=(not sem_add) or c == 1)
                ins.then_inc(st_full, 1)

            def values_product(s, j):
                l = layer(s)
                rows, buf = HROWS[l], vals[PATTERN[l]]
                if j == 0:
                    pe.wait_ge(vals_marked, 2 if l == 3 else 1)
                    taken(pe, last_values_hop(s))
                pe.wait_ge(probs_ready, st_count(s, 4 * j + 3))
                n = s * QUADS + j
                if n:
                    pe.wait_ge(outT_ready, n)
                per = P // rows
                for g in range(4 // per):
                    for c in range(KT):
                        for i in range(per):
                            h = 4 * j + g * per + i
                            ins = mm(bank[4][i * rows:(i + 1) * rows, g * S:(g + 1) * S],
                                     buf[:, s % 2, c, h, :], probs[:, h % 8, c, :],
                                     start=(c == 0), stop=(c == 1))
                ins.then_inc(o_full, 1)

            def text_product(s, heads):
                for h in heads:
                    n = s * H + h
                    if n >= 2:
                        pe.wait_ge(y_free, n - 1)
                    elif n == 0:
                        pe.wait_ge(hop_taken[6], plan.hops_on_6_before_text)
                    out = bank[6 + n % 2]
                    for qt in range(QT):
                        for c in range(KT):
                            ins = mm(out[:, qt * E:(qt + 1) * E], probs[:, h % 8, c, qt * P:(qt + 1) * P],
                                     text[:, KT * batch(s) + c, :], start=(c == 0), stop=(c == KT - 1))
                    ins.then_inc(y_full, 1)

            def project(out, w, src, cols):
                for half in range(2):
                    for k in range(2):
                        ins = mm(out[0:HALF, half * cols:(half + 1) * cols], w[:, k, half * HALF:(half + 1) * HALF],
                                 src[:, k, :], start=(k == 0), stop=(k == 1))
                return ins

            def hop(key):
                kind, s = key[0], key[1]
                l, b = layer(s), batch(s)
                if kind == "NORM":
                    pe.wait_ge(ones_ready, 1)
                    pe.wait_ge(ipsq_ready, 1)
                    out = begin(key)
                    for e in range(2):
                        ins = mm(out[:, 0:B * NIP0], ones[:], ipsq[:, e].rearrange("p b n -> p (b n)"),
                                 start=(e == 0), stop=(e == 1))
                elif kind == "K":
                    if l == 0:
                        pe.wait_ge(loaded_ctx[b], 16)
                    if b == 0:
                        pe.wait_ge(loaded_wk[l], 16)
                    out = begin(key)
                    for half in range(2):
                        for g, (a, z) in enumerate(SEGS[l]):
                            for e in range(2):
                                ins = mm(out[0:HALF, half * T + a:half * T + z],
                                         wk[l][:, g, e, half * HALF:(half + 1) * HALF],
                                         ctxT[:, e, b * T + a:b * T + z], start=(e == 0), stop=(e == 1))
                elif kind == "Q":
                    if s == 0:
                        pe.wait_ge(loaded_x, 16 * 2)
                    if s >= B:
                        taken(pe, ("OUT", s - B))
                    out = begin(key)
                    ins = project(out, wq[:, l], xT[:, :, b * S:(b + 1) * S], S)
                elif kind == "M":
                    pe.wait_ge(maxsplit_ready, s + 1)
                    out = begin(key)[:].bitcast(BF16)
                    n = 3 * len(SEGS[l]) * H
                    for qt in range(QT):
                        flat = maxsplit[:, qt].rearrange("p a n -> p (a n)")
                        for k in range(n // 120):
                            ins = nc.tensor.transpose(out[0:120, k * S + qt * P:k * S + (qt + 1) * P],
                                                      flat[:, k * 120:(k + 1) * 120], identb[:])
                elif kind == "T":
                    _, _, n, qt = key
                    units = t_rounds(l)[n]
                    per = 4 * HROWS[l] // P
                    pe.wait_ge(outT_ready, s * QUADS + units[-1] // per + 1)
                    out = begin(key)
                    for i, u in enumerate(units):
                        ins = nc.tensor.transpose(out[:, i * P:(i + 1) * P], outT[:, u, qt * P:(qt + 1) * P],
                                                  ident[:])
                elif kind == "AT":
                    pe.wait_ge(attn_ready, s + 1)
                    out = begin(key)
                    for half in range(2):
                        for qt in range(QT):
                            ins = nc.tensor.transpose(out[0:HALF, half * S + qt * P:half * S + (qt + 1) * P],
                                                      attn[:, qt, half * HALF:(half + 1) * HALF], ident[:])
                elif kind == "OUT":
                    taken(pe, ("AT", s))
                    out = begin(key)
                    ins = project(out, wo[:, l], attnT[:], S)
                elif kind == "V":
                    if b == 0:
                        pe.wait_ge(loaded_w[l], 16)
                    if s == 0:
                        pe.wait_ge(loaded_const, 16 * 6)
                    out = begin(key)
                    for i, (c, g) in enumerate(v_parts(l)[key[2]]):
                        for e in range(2):
                            ins = mm(out[:, i * C:(i + 1) * C], ctxT[:, e, b * T + c * P:b * T + (c + 1) * P],
                                     wv[l][:, g, e, :], start=(e == 0), stop=(e == 1))
                    if l == 0:
                        for c in range(KT):
                            for e in range(2):
                                ins = mm(out[:, 2 * C + c * NIP0:2 * C + (c + 1) * NIP0],
                                         ctxT[:, e, b * T + c * P:b * T + (c + 1) * P],
                                         ctxT[:, e, (b + 1) * T - NIP0:(b + 1) * T], start=(e == 0), stop=(e == 1))
                elif kind == "VIP":
                    out = begin(key)
                    for i in range(3 if key[2] == 0 else 1):
                        col = (b + 1) * T - NIP0 + 3 * key[2] + i
                        for e in range(2):
                            ins = mm(out[:, i * C:(i + 1) * C], ctxT[:, e, col:col + 1].broadcast_to([P, P]),
                                     wv[0][:, 1, e, :], start=(e == 0), stop=(e == 1))
                elif kind == "FULL":
                    out = begin(key)
                    for e in range(2):
                        mm(out[0:NTEXT, 0:T - NTEXT], ctxT[:, e, b * T:b * T + NTEXT],
                           ctxT[:, e, b * T + NTEXT:(b + 1) * T], start=(e == 0), stop=(e == 1))
                    pe.wait_ge(full_ready, 2 * (b + 1))
                    for qt in range(QT):
                        for k in range(2):
                            ins = mm(out[:, 256 + qt * NTEXT:256 + (qt + 1) * NTEXT], qfull[:, k, qt * P:(qt + 1) * P],
                                     kfull[:, k, :], start=(k == 0), stop=(k == 1))
                elif kind == "PT":
                    pe.wait_ge(pfull_ready, b + 1)
                    out = begin(key)
                    for qt in range(QT):
                        ins = nc.tensor.transpose(out[0:NTEXT, qt * P:(qt + 1) * P], pfull[:, 1, qt, :], ident[:])
                elif kind == "SEM":
                    taken(pe, ("PT", s))
                    out = begin(key)
                    for qt in range(QT):
                        ins = mm(out[:, qt * T:(qt + 1) * T], pfullT[:, qt * P:(qt + 1) * P], textip[:],
                                 start=True, stop=True)
                elif kind == "SEMT":
                    out = begin(key)
                    for c in range(KT):
                        ins = mm(out[:, c * S:(c + 1) * S], textip[:, c * P:(c + 1) * P], pfullT[:],
                                 start=True, stop=True)
                ins.then_inc(hop_full, 1)

            for s in range(FIRST, LAST + 1):
                at = hops(s)
                exp = 0 <= s < SLOTS
                for j in range(QUADS):
                    a, k = score_quad(s, j)
                    if exp:
                        scores_for_exp(s, 4 * j)
                        scores_for_exp(s, 4 * j + 1)
                    if 0 <= a < SLOTS:
                        scores_for_max(a, k, 0)
                        scores_for_max(a, k, 1)
                    if exp and j:
                        values_product(s, j - 1)
                        if layer(s) == 0:
                            if s == 0 and j == 1:
                                pe.wait_ge(text_masked, 1)
                            text_product(s, quad_heads(j - 1)[0:2])
                    for key in at[2 * j + MID]:
                        hop(key)
                    if exp:
                        scores_for_exp(s, 4 * j + 2)
                        scores_for_exp(s, 4 * j + 3)
                    if 0 <= a < SLOTS:
                        scores_for_max(a, k, 2)
                        scores_for_max(a, k, 3)
                    if exp and j and layer(s) == 0:
                        text_product(s, quad_heads(j - 1)[2:4])
                    for key in at[2 * j + END]:
                        hop(key)
                for key in at[TAIL]:
                    hop(key)
                if exp:
                    values_product(s, QUADS - 1)
                    if layer(s) == 0:
                        text_product(s, quad_heads(QUADS - 1))

        @block.scalar
        def _(act):
            def copy(out, in_, scale=None):
                if scale is None:
                    return nc.scalar.activation(out, in_, ACT.Copy)
                return nc.scalar.activation(out, in_, ACT.Copy, scale=scale)

            def exponentials(s, h):
                n = s * H + h
                act.wait_ge(st_full, n + 1)
                if n >= 8 and h % 4 == 0:
                    q = s * QUADS + h // 4
                    act.wait_ge(o_full, q - 1)
                    if q - 1 <= B * QUADS:
                        act.wait_ge(y_full, 4 * (q - 1))
                    elif q - 2 < B * QUADS:
                        act.wait_ge(y_full, B * H)
                nc.scalar.activation(probs[:, h % 8].rearrange("p c q -> p (c q)"), bank[n % 2][:], ACT.Exp,
                                     scale=SCALE).then_inc(probs_ready, 1)

            def take_out(s, j):
                l = layer(s)
                n = s * QUADS + j
                per = 4 * HROWS[l] // P
                if j == 0 and s >= 1:
                    last = t_rounds(layer(s - 1))
                    act.wait_ge(hop_full, full_of(("T", s - 1, len(last) - 1, QT - 1)))
                act.wait_ge(o_full, n + 1)
                copy(outT[:, per * j:per * (j + 1), :],
                     bank[4][:, 0:per * S].rearrange("p (u q) -> p u q", u=per)).then_inc(outT_ready, 1)

            def square_norms(s, heads):
                for h in heads:
                    n = s * H + h
                    act.wait_ge(y_full, n + 1)
                    for qt in range(QT):
                        y = bank[6 + n % 2][:, qt * E:(qt + 1) * E]
                        ins = nc.scalar.activation(y, y, ACT.Square, accum_out=norm2[:, s % 2, qt, h:h + 1])
                    ins.then_inc(y_free, 1)

            def hop(key):
                kind, s = key[0], key[1]
                l, b = layer(s), batch(s)
                n, hb, _ = plan.hop[key]
                src = bank[hb]
                if kind == "NORM":
                    taken(act, key)
                    nc.scalar.activation(ipn[:, 1], ipn[:, 0], ACT.Sqrt).then_inc(root_ready, 1)
                elif kind in ("K", "Q"):
                    act.wait_ge(hop_full, n + 1)
                    dst, stored = (ksplit, k_stored) if kind == "K" else (qsplit, q_stored)
                    if s:
                        act.wait_ge(stored, 16 * s)
                    if l == 1:
                        if kind == "K":
                            if b:
                                act.wait_ge(hop_full, full_of(("FULL", s - 1)))
                            copy(kfull[:], src[0:HALF].rearrange("p (h t) -> p h t", h=2)[:, :, 0:NTEXT])\
                                .then_inc(full_ready, 1)
                        else:
                            copy(qfull[:].rearrange("p h q -> p (h q)"), src[0:HALF]).then_inc(full_ready, 1)
                    copy(dst[:, 0].rearrange("p h t -> p (h t)"), src[0:HALF]).then_inc(high_ready, 1)
                elif kind == "M":
                    act.wait_ge(hop_full, n + 1)
                    if s:
                        act.wait_ge(m_stored, 16 * s)
                    nblk = 3 * len(SEGS[l]) * H // 120
                    copy(maxT[:, 0:nblk].rearrange("p n q -> p (n q)"), src[:].bitcast(BF16)[0:120, 0:nblk * S])\
                        .then_inc(hop_taken[hb], 1)
                elif kind == "T" and l == 0 and key[2:] == (len(t_rounds(0)) - 1, QT - 1):
                    act.wait_ge(norm_ready, s + 1)
                    nc.scalar.activation(nrm[:, 2], nrm[:, 1], ACT.Sqrt).then_inc(root_ready, 1)
                    act.wait_ge(fused_ready, s + 1)
                    nc.scalar.activation(fused[:, 2], fused[:, 1], ACT.Exp, scale=SCALE).then_inc(fexp_ready, 1)
                elif kind == "AT":
                    act.wait_ge(hop_full, n + 1)
                    copy(attnT[:].rearrange("p h q -> p (h q)"), src[0:HALF]).then_inc(hop_taken[hb], 1)
                elif kind == "V":
                    act.wait_ge(hop_full, n + 1)
                    buf = vals[PATTERN[l]]
                    if key[2] == 0:
                        act.wait_ge(vals_zeroed, 3 if l == 3 else 2)
                        if s >= 2:
                            act.wait_ge(o_full, (s - 1) * QUADS)
                    for i, (c, g) in enumerate(v_parts(l)[key[2]]):
                        ins = copy(buf[:, s % 2, c, :, 9 * g:9 * g + D],
                                   src[:, i * C:(i + 1) * C].rearrange("p (h d) -> p h d", h=H),
                                   segmask[:, PATTERN[l], c, g:g + 1])
                    if l == 0:
                        for c in range(KT):
                            ins = copy(buf[:, s % 2, c, :, 9:9 + NIP0],
                                       src[:, 2 * C + c * NIP0:2 * C + (c + 1) * NIP0].unsqueeze(1)
                                       .broadcast_to([P, H, NIP0]), segmask[:, 0, c, 0:1])
                    ins.then_inc(hop_taken[hb], 1)
                elif kind == "VIP":
                    act.wait_ge(hop_full, n + 1)
                    if s >= 2 and key[2] == 0:
                        act.wait_ge(attn_ready, s - 1)
                    m = 3 if key[2] == 0 else 1
                    copy(v_ip[:, s % 2, 3 * key[2]:3 * key[2] + m, :],
                         src[:, 0:m * C].rearrange("p (n c) -> p n c", n=m)).then_inc(hop_taken[hb], 1)
                elif kind == "FULL":
                    act.wait_ge(hop_full, n + 1)
                    if b:
                        act.wait_ge(hop_full, full_of(("SEMT", s - 1)))
                    copy(textip[:, NTEXT:T], src[0:NTEXT, 0:T - NTEXT]).then_inc(textip_ready, 1)
                    act.wait_ge(bias_ready, b + 1)
                    for qt in range(QT):
                        ins = nc.scalar.activation(pfull[:, 0, qt, :], src[:, 256 + qt * NTEXT:256 + (qt + 1) * NTEXT],
                                                   ACT.Exp, bias=fstat[:, 1, qt:qt + 1], scale=SCALE,
                                                   accum_out=fstat[:, 2, qt:qt + 1])
                    ins.then_inc(hop_taken[hb], 1)
                elif kind == "PT":
                    act.wait_ge(hop_full, n + 1)
                    copy(pfullT[:], src[0:NTEXT, 0:S]).then_inc(hop_taken[hb], 1)
                elif kind == "SEM":
                    act.wait_ge(hop_full, n + 1)
                    if b >= 2:
                        act.wait_ge(s_free, (s - 1) * 4 * QUADS)
                    copy(semq[:, s % 2], src[:], 0.5).then_inc(hop_taken[hb], 1)
                elif kind == "SEMT":
                    act.wait_ge(hop_full, n + 1)
                    if b == 3:
                        act.wait_ge(st_full, st_count(s - 3, H - 1))
                    copy(semk[:, s % 3, 0], src[:], 0.5).then_inc(high_ready, 1)

            for s in range(FIRST, LAST + 1):
                at = hops(s)
                exp = 0 <= s < SLOTS
                if s == -1:
                    act.wait_ge(loaded_const, 16 * 6)
                for j in range(QUADS):
                    if exp:
                        exponentials(s, 4 * j)
                        exponentials(s, 4 * j + 1)
                        if j:
                            take_out(s, j - 1)
                            if layer(s) == 0:
                                if j == 1 and s >= 2:
                                    act.wait_ge(attn_ready, s - 1)
                                square_norms(s, quad_heads(j - 1)[0:2])
                    for key in at[2 * j + MID]:
                        hop(key)
                    if exp:
                        exponentials(s, 4 * j + 2)
                        exponentials(s, 4 * j + 3)
                        if j and layer(s) == 0:
                            square_norms(s, quad_heads(j - 1)[2:4])
                    for key in at[2 * j + END]:
                        hop(key)
                for key in at[TAIL]:
                    hop(key)
                if exp:
                    take_out(s, QUADS - 1)
                    if layer(s) == 0:
                        square_norms(s, quad_heads(QUADS - 1))

        @block.vector
        def _(dve):
            steps = [0]

            def link(ins):
                steps[0] += 1
                ins.then_inc(dve_step, 1)
                dve.wait_ge(dve_step, steps[0])

            tt, ts, stt = nc.vector.tensor_tensor, nc.vector.tensor_scalar, nc.vector.scalar_tensor_tensor

            def maxima(a, j, u):
                qt, half = heads_of(u)
                n, b, _ = plan.unit[(a, j, u)]
                l = layer(a)
                if j == 0 and u == 0 and a >= 2:
                    dve.wait_ge(maxsplit_ready, a - 1)
                dve.wait_ge(s_full, n + 1)
                src = bank[b][:].rearrange("p (s t) -> p s t", s=2)
                dst = negmax[:, a % 2, qt, 0:len(SEGS[l]) * H]\
                    .rearrange("p (g e s) -> p s g e", g=len(SEGS[l]), e=2)[:, 2 * j:2 * j + 2, :, half]

                if l == 1 and j == 0 and u == 0:
                    taken(dve, ("SEM", a))

                def take(g, z):
                    lo, hi = SEGS[l][g][0], SEGS[l][z - 1][1]
                    return nc.vector.tensor_reduce(
                        dst[:, :, g:z], src[:, :, lo:hi].rearrange("p s (g k) -> p s g k", g=z - g),
                        AX.X, ALU.max, negate=True)
                if l == 0:
                    nc.vector.tensor_copy(
                        s_ip[:, batch(a), qt].rearrange("p (s e) n -> p s e n", e=2)[:, 2 * j:2 * j + 2, half, :],
                        src[:, :, T - NIP0:T])
                runs = {0: [(0, 1), (1, 2)], 1: [(0, 1)], 2: [(0, 1), (1, 2)], 3: [(0, 1), (1, 3), (3, 4)]}[l]
                for g, z in runs:
                    ins = take(g, z)
                if l == 1:
                    lo = SEGS[1][1][0]
                    for i in range(2):
                        x = src[:, i, lo:T]
                        ins = nc.vector.tensor_tensor_reduce(
                            out=x, in0=x, in1=semq[:, a % 2, qt * T + lo:(qt + 1) * T], scale=-1.0,
                            scalar=3.0e38, op0=ALU.add, op1=ALU.min, accum_out=dst[:, i, 1:2])
                ins.then_inc(s_free, 1)

            def image_keys(s):
                b = batch(s)
                dve.wait_ge(y_free, (s + 1) * H)
                link(tt(nrm[:, 0], norm2[:, s % 2], rsum[:, :, :, 0], ALU.mult))
                link(tt(nrm[:, 3], nrm[:, 0], rsum[:, :, :, 0], ALU.mult))
                nc.vector.tensor_scalar_max(nrm[:, 1], nrm[:, 3], EPS2).then_inc(norm_ready, 1)
                dve.wait_ge(root_ready, s + 2)
                link(nc.vector.reciprocal(fsum[:, 0], nrm[:, 2]))
                link(tt(fused[:, 0], dots[:], fsum[:, 0].unsqueeze(3).broadcast_to([P, QT, H, NIP0]), ALU.mult))
                link(tt(fused[:, 1].rearrange("p q h n -> p (q h) n"), fused[:, 0].rearrange("p q h n -> p (q h) n"),
                        ipn[:, 2, b].unsqueeze(1).broadcast_to([P, QT * H, NIP0]), ALU.mult))
                link(stt(fused[:, 0].rearrange("p q h n -> p (q h n)"), fused[:, 1].rearrange("p q h n -> p (q h n)"),
                         0.5 / SCALE, s_ip[:, b].rearrange("p q h n -> p (q h n)"), ALU.mult, ALU.add))
                link(nc.vector.tensor_reduce(fsum[:, 1], fused[:, 0], AX.X, ALU.max))
                tt(fused[:, 1], fused[:, 0], fsum[:, 1].unsqueeze(3).broadcast_to([P, QT, H, NIP0]), ALU.subtract)\
                    .then_inc(fused_ready, 1)
                dve.wait_ge(fexp_ready, s + 1)
                link(nc.vector.tensor_reduce(fsum[:, 2], fused[:, 2], AX.X, ALU.add))
                link(nc.vector.reciprocal(fsum[:, 3], fsum[:, 2]))
                link(tt(fsum[:, 4], fsum[:, 3], spatial[:].unsqueeze(2).broadcast_to([P, QT, H]), ALU.mult))
                link(tt(fused[:, 0], fused[:, 2], fsum[:, 4].unsqueeze(3).broadcast_to([P, QT, H, NIP0]), ALU.mult))
                taken(dve, ("VIP", s, 1))
                for qt in range(QT):
                    for n in range(NIP0):
                        ins = tt(ipprod[:, n].rearrange("p (h d) -> p h d", h=H),
                                 v_ip[:, s % 2, n].rearrange("p (h d) -> p h d", h=H),
                                 fused[:, 0, qt, :, n].unsqueeze(2).broadcast_to([P, H, D]), ALU.mult)
                    link(ins)
                    link(nc.vector.tensor_reduce(ipout[:], ipprod[:].rearrange("p n c -> p c n"), AX.X, ALU.add))
                    ins = tt(attn[:, qt], ipout[:], attn[:, qt], ALU.add)
                    if qt < QT - 1:
                        link(ins)
                ins.then_inc(attn_ready, 1)

            def hop(key):
                kind, s = key[0], key[1]
                l, b = layer(s), batch(s)
                n, hb, before = plan.hop[key]
                src = bank[hb]
                if kind == "NORM":
                    dve.wait_ge(hop_full, n + 1)
                    nc.vector.tensor_scalar_max(ipn[:, 0].rearrange("p b n -> p (b n)"), src[:, 0:B * NIP0], EPS2)\
                        .then_inc(hop_taken[hb], 1)
                    dve.wait_ge(root_ready, 1)
                    link(nc.vector.reciprocal(ipn[:, 2], ipn[:, 1]))
                elif kind in ("K", "Q", "SEMT"):
                    i = plan.split[key]
                    dve.wait_ge(high_ready, i + 1)
                    if i:
                        dve.wait_ge(split_ready, i)
                    if kind in ("K", "Q"):
                        parts = (ksplit if kind == "K" else qsplit)[:].rearrange("p a h t -> p a (h t)")
                        left = rest[0:HALF, 0]
                        ins = tt(left, src[0:HALF], parts[:, 0], ALU.subtract)
                    else:
                        parts, left = semk[:, s % 3], rest[:, 0]
                        ins = stt(left, src[:], 0.5, parts[:, 0], ALU.mult, ALU.subtract)
                    ins.then_inc(hop_taken[hb], 1)
                    taken(dve, key)
                    nc.vector.tensor_copy(parts[:, 1], left).then_inc(rest_ready, 1)
                elif kind == "T":
                    _, _, rnd, qt = key
                    dve.wait_ge(hop_full, n + 1)
                    units = t_rounds(l)[rnd]
                    per = P // HROWS[l]
                    h0, h1 = units[0] * per, (units[-1] + 1) * per
                    nh, g = h1 - h0, 1 if l == 0 else len(SEGS[l])
                    view = tr_view(l, key, units)
                    if rnd == 0 and qt == 0 and s:
                        dve.wait_ge(hop_full, full_of(("AT", s - 1)))
                    if l == 0:
                        link(nc.vector.reciprocal(rsum[:, qt, h0:h1, 0], view[:, :, D]))
                        tt(attn[:, qt, h0 * D:h1 * D].rearrange("p (h d) -> p h d", h=nh), view[:, :, 0:D],
                           rsum[:, qt, h0:h1, 0:1].broadcast_to([P, nh, D]), ALU.mult)
                        tt(dots[:, qt, h0:h1], view[:, :, 9:9 + NIP0],
                           rsum[:, qt, h0:h1, 0:1].broadcast_to([P, nh, NIP0]), ALU.mult).then_inc(hop_taken[hb], 1)
                        if (rnd, qt) == (len(t_rounds(0)) - 1, QT - 1):
                            taken(dve, key)
                            image_keys(s)
                    else:
                        parts = view[:, :, 0:9 * g].rearrange("p h (g k) -> p h g k", k=9)
                        link(nc.vector.reciprocal(rsum[:, qt, h0:h1, 0:g], parts[:, :, :, D]))
                        if l == 1:
                            link(ts(rsum[:, qt, h0:h1, 1], rsum[:, qt, h0:h1, 1], spatial[:, qt:qt + 1], None, ALU.mult))
                        tt(scaled[:, 0:nh, 0:g], parts[:, :, :, 0:D],
                           rsum[:, qt, h0:h1, 0:g].unsqueeze(3).broadcast_to([P, nh, g, D]), ALU.mult)\
                            .then_inc(hop_taken[hb], 1)
                        taken(dve, key)
                        ins = nc.vector.tensor_reduce(attn[:, qt, h0 * D:h1 * D].rearrange("p (h d) -> p h d", h=nh),
                                                      scaled[:, 0:nh, 0:g].rearrange("p h g d -> p h d g"),
                                                      AX.X, ALU.add)
                        if (rnd, qt) == (len(t_rounds(l)) - 1, QT - 1):
                            ins.then_inc(attn_ready, 1)
                        else:
                            link(ins)
                elif kind == "OUT":
                    dve.wait_ge(hop_full, n + 1)
                    for half in range(2):
                        x = xT[:, half, b * S:(b + 1) * S]
                        ins = stt(x, src[0:HALF, half * S:(half + 1) * S], bo[:, l, half:half + 1], x, ALU.add, ALU.add)
                    ins.then_inc(hop_taken[hb], 1)
                elif kind == "FULL":
                    dve.wait_ge(textip_ready, b + 1)
                    link(nc.vector.tensor_reduce(fstat[:, 0], src[:, 256:256 + QT * NTEXT]
                                                 .rearrange("p (q t) -> p q t", q=QT), AX.X, ALU.max, negate=True))
                    ts(fstat[:, 1], fstat[:, 0], SCALE, None, ALU.mult).then_inc(bias_ready, 1)
                    taken(dve, key)
                    link(nc.vector.reciprocal(fstat[:, 3], fstat[:, 2]))
                    for qt in range(QT):
                        ins = ts(pfull[:, 1, qt], pfull[:, 0, qt], fstat[:, 3, qt:qt + 1], None, ALU.mult)
                    ins.then_inc(pfull_ready, 1)

            dve.wait_ge(ones_ready, 1)

            def mark_segments(zeroed, patterns):
                dve.wait_ge(vals_zeroed, zeroed)
                for pattern, segs in patterns:
                    for c in range(KT):
                        for g in range(segs):
                            ins = ts(vals[pattern][:, :, c, :, 9 * g + D],
                                     ones[:, 0:2 * H].rearrange("p (i h) -> p i h", i=2),
                                     segmask[:, pattern, c, g:g + 1], None, ALU.mult)
                ins.then_inc(vals_marked, 1)

            for b in range(B):
                dve.wait_ge(loaded_ctx[b], 16)
            ip = ctxT[:].rearrange("p e (b t) -> p e b t", b=B)[:, :, :, T - NIP0:T]
            for e in range(2):
                ins = tt(ipsq[:, e], ip[:, e], ip[:, e], ALU.mult)
            ins.then_inc(ipsq_ready, 1)
            for s in range(FIRST, LAST + 1):
                at = hops(s)
                if s == -1:
                    dve.wait_ge(loaded_const, 16 * 6)
                    mark_segments(2, ((0, 1), (1, 2)))
                if s == 0:
                    dve.wait_ge(loaded_text, 16)
                    odd = text[:].rearrange("p (b c) e -> p c b e", c=KT)[:, 1]
                    ts(odd, odd, segmask[:, 0, 1, 0:1], None, ALU.mult).then_inc(text_masked, 1)
                for j in range(QUADS):
                    a, k = score_quad(s, j)
                    for half in (MID, END):
                        if 0 <= a < SLOTS:
                            maxima(a, k, 2 * half)
                            maxima(a, k, 2 * half + 1)
                        for key in at[2 * j + half]:
                            hop(key)
                for key in at[TAIL]:
                    hop(key)
                if s == 7:
                    mark_segments(3, ((2, 4),))

        @block.gpsimd
        def _(pool):
            steps = [0]

            def link(ins):
                steps[0] += 1
                ins.then_inc(pool_step, 1)
                pool.wait_ge(pool_step, steps[0])

            nc.gpsimd.memset(ones[:], 1.0).then_inc(ones_ready, 1)
            for v in (vals_wide, vals_mid):
                nc.gpsimd.memset(v[:], 0.0).then_inc(vals_zeroed, 1)
            nc.gpsimd.memset(textip[:, 0:NTEXT], 0.0).then_inc(ones_ready, 1)

            def lower_parts(key):
                kind, s = key[0], key[1]
                i = plan.split[key]
                pool.wait_ge(rest_ready, i + 1)
                if kind in ("K", "Q"):
                    dst = [(ksplit if kind == "K" else qsplit)[:, p].rearrange("p h t -> p (h t)") for p in (1, 2)]
                    src = rest[0:HALF, 0]
                else:
                    buf = semk[:, s % 3]
                    dst, src = [buf[:, 1], buf[:, 2]], rest[:, 0]
                nc.gpsimd.tensor_tensor(dst[1], src, dst[0], ALU.subtract).then_inc(split_ready, 1)

            def split_maxima(a):
                n = len(SEGS[layer(a)]) * H
                pool.wait_ge(s_free, (a + 1) * 4 * QUADS)
                if a:
                    pool.wait_ge(hop_full, full_of(("M", a - 1)))
                src, left = negmax[:, a % 2, :, 0:n], maxrest[:, :, 0:n]
                flat = maxsplit[:].rearrange("p q a n -> p q (a n)")
                part = [flat[:, :, p * n:(p + 1) * n] for p in range(3)]
                link(nc.gpsimd.tensor_copy(part[0], src))
                link(nc.gpsimd.tensor_tensor(left, src, part[0], ALU.subtract))
                link(nc.gpsimd.tensor_copy(part[1], left))
                nc.gpsimd.tensor_tensor(part[2], left, part[1], ALU.subtract).then_inc(maxsplit_ready, 1)

            for s in range(FIRST, LAST + 1):
                for pos, keys in enumerate(hops(s)):
                    if pos == 5 and 0 <= s + 1 < SLOTS:
                        split_maxima(s + 1)
                    for key in keys:
                        if key in plan.split:
                            lower_parts(key)
                if s == 6:
                    pool.wait_ge(o_full, B * QUADS)
                    nc.gpsimd.memset(vals_wide[:], 0.0).then_inc(vals_zeroed, 1)


def kernel(**inputs):
    import ml_dtypes
    import numpy as np
    import concourse.bacc as bacc
    from concourse.bass_utils import run_bass_kernel_spmd as run

    f = lambda name: np.asarray(inputs[name])

    def by_half(w):
        return w.reshape(w.shape[0], NS, 2, D).transpose(0, 2, 3, 1).reshape(w.shape[0], C)

    def rows(w):
        n = HALF if w.shape[0] == C else P
        return w.reshape(-1, n, w.shape[1]).transpose(1, 0, 2)

    names = [
        dict(q="L0_xattn_W_q", k=["L0_xattn_W_k", "L0_xattn_W_k_ip"], v=["L0_xattn_W_v", "L0_xattn_W_v_ip"],
             o="L0_xattn_W_out", b="L0_xattn_b_out"),
        dict(q="L1_xattn_Wq", k=["L1_xattn_Wk", "L1_xattn_Wk_ip"], v=["L1_xattn_Wv", "L1_xattn_Wv_ip"],
             o="L1_xattn_Wout", b="L1_xattn_bout"),
        dict(q="L2_xattn_Wq", k=["L2_xattn_Wk", "L2_xattn_Wk_ip"], v=["L2_xattn_Wv", "L2_xattn_Wv_ip"],
             o="L2_xattn_Wo", b="L2_xattn_bo"),
        dict(q="L3_xattn_to_q_w", k=[f"L3_xattn_to_k_{x}w" for x in ("", "object_", "others_", "ip_")],
             v=[f"L3_xattn_to_v_{x}w" for x in ("", "object_", "others_", "ip_")],
             o="L3_xattn_to_out_w", b="L3_xattn_to_out_b"),
    ]
    w = lambda l, name: f(name).T if l == 2 else f(name)
    arrays = {
        "xT": f("x").reshape(B * S, 2, HALF).transpose(2, 1, 0),
        "ctxT": f("ctx_2048").reshape(B * T, 2, P).transpose(2, 1, 0),
        "text": f("ctx_2048").reshape(B * KT, P, E).transpose(1, 0, 2),
        "spatial": f("fside_S_0").reshape(QT, P).T,
        "wq": np.stack([rows(by_half(w(l, n["q"]))) for l, n in enumerate(names)], 1),
        "wo": np.stack([rows(w(l, n["o"])) for l, n in enumerate(names)], 1),
        "bo": np.stack([f(n["b"]).reshape(2, HALF).T for n in names], 1),
    }
    for l, n in enumerate(names):
        arrays[f"wk{l}"] = np.stack([rows(by_half(w(l, x))) for x in n["k"]], 1)
        arrays[f"wv{l}"] = np.stack([rows(w(l, x)) for x in n["v"]], 1)
    masks = np.zeros((P, 3, KT, 4), np.float32)
    for l in (0, 1, 3):
        marks = np.zeros((len(SEGS[l]), T), np.float32)
        for g, (a, z) in enumerate(SEGS[l]):
            marks[g, a:z] = 1
            masks[:, PATTERN[l], :, g] = marks[g].reshape(KT, P).T
        arrays[f"marks{PATTERN[l]}"] = np.tile(marks, (3, NS)).astype(ml_dtypes.bfloat16)
    arrays["segmask"] = masks
    arrays["ident"] = np.eye(P, dtype=np.float32)
    arrays["identb"] = np.eye(P, dtype=np.float32).astype(ml_dtypes.bfloat16)

    nc = bacc.Bacc("TRN2", target_bir_lowering=False, num_devices=1)
    arrays = {f"in_{k}": np.ascontiguousarray(a) for k, a in arrays.items()}
    t = {k[3:]: nc.dram_tensor(k, a.shape, mybir.dt.from_np(a.dtype), kind="ExternalInput").ap()
         for k, a in arrays.items()}
    t["out"] = nc.dram_tensor("out", (HALF, 2, B * S), F32, kind="ExternalOutput").ap()
    program(nc, t)
    r = run(nc, [arrays], core_ids=[0])
    return r.results[0]["out"].transpose(2, 1, 0).reshape(B, S, C)
```

```python
from contextlib import ExitStack

import concourse.bass as bass
from concourse import mybir

F32 = mybir.dt.float32
BF16 = mybir.dt.bfloat16
ACT = mybir.ActivationFunctionType
ALU = mybir.AluOpType
AX = mybir.AxisListType

P = 128
B, S, C, E, T = 4, 256, 160, 256, 256
H, D = 20, 8
NL = 4
SLOTS = NL * B
SCALE = float(D) ** -0.5
HALF = C // 2
QUADS = H // 4
NS = H // 2
NPROD = 6
PARTS = {"K": (0, 1, 2), "Q": (1, 2, 0)}
CONSTANTS = 5
ROWS = NPROD * D
QT = S // P
KT = T // P
EPS2 = 1e-24

SEGS = [
    [(0, 252), (252, 256)],
    [(0, 77), (77, 256)],
    [(0, 77), (77, 256)],
    [(0, 77), (77, 81), (81, 85), (85, 256)],
]
NTEXT = 77
PATTERN = [0, 1, 1, 2]
HROWS = [32, 32, 32, 64]
NIP0 = 4


def layer(s):
    return s // B


def batch(s):
    return s % B


def v_parts(l):
    segs = SEGS[l][:1] if l == 0 else SEGS[l]
    pairs = [(c, g) for c in range(KT) for g, (a, z) in enumerate(segs) if a < (c + 1) * P and z > c * P]
    return [pairs[i:i + 3] for i in range(0, len(pairs), 3)]


def t_rounds(l):
    units = H * HROWS[l] // P
    n = 3 if l < 3 else 4
    return [list(range(i, min(i + n, units))) for i in range(0, units, n)]


def score_quad(s, j):
    g = s * QUADS + j - 2
    return g // QUADS + 2, g % QUADS


def behind(s, h):
    if h >= 4:
        return (s, h - 4) if 0 <= s < SLOTS else None
    return (s - 1, H + h - 4) if s >= 1 and s - 1 not in (B - 1, SLOTS - 1) else None


def values_step(s):
    return 1 if s < B else 2


LONG = ("K", "Q", "V", "OUT")

PLACES = {
    "filling": dict(K=[1], Q=[4]),
    "before": dict(K=[1], M=[14], NORM=[12], V=[9], VIP=[12], Q=[15]),
    "text": dict(FULL=[0], PT=[5], K=[2], LATE=[3, 5], SEM=[8], SEMT=[9], V=[11], M=[13], AT=[12], OUT=[15],
                 EARLY=[16, 19], Q=[18]),
    "after text": dict(FULL=[0], PT=[1], K=[1], LATE=[2, 3], SEM=[5], SEMT=[7], V=[11], M=[14], AT=[14], OUT=[16],
                       EARLY=[17, 18], Q=[18]),
    "steered": dict(FULL=[0], PT=[2], K=[1], LATE=[4, 4], SEM=[3], SEMT=[6], V=[14, 18], M=[13], AT=[7], OUT=[10],
                    EARLY=[16, 18], Q=[17]),
    "plain": dict(K=[2], LATE=[4, 5], V=[13, 16], M=[14], AT=[9], OUT=[13], EARLY=[16, 18], Q=[17]),
    "wide": dict(K=[5], LATE=[4, 4, 6, 6], V=[12, 14], M=[10], AT=[9], OUT=[13], EARLY=[16, 16], Q=[16]),
}
SPLIT_MAXIMA = {
    "before": [8, 8, 9, 9],
    "text": [8, 9, 9, 12],
    "after text": [8, 9, 10, 12],
    "steered": [8, 8, 9, 11],
    "plain": [8, 9, 9, 11],
    "wide": [8, 9, 9, 9],
}


def regime(s):
    if s < 0:
        return "filling" if s < -1 else "before"
    if s <= B:
        return "text" if s < B else "after text"
    if s < 2 * B:
        return "steered"
    return "plain" if s <= 3 * B else "wide"


def hops(s):
    at = [[] for _ in range(H)]
    ahead, next2, following, now, last = [x if 0 <= x < SLOTS else None for x in (s + 3, s + 2, s + 1, s, s - 1)]
    keys = {}
    if ahead is not None:
        keys["K"] = [("K", ahead)]
        keys["Q"] = [("Q", ahead)]
    if next2 is not None and layer(next2) == 1:
        for kind in ("FULL", "PT", "SEM", "SEMT"):
            keys[kind] = [(kind, next2)]
    if last is not None:
        keys["LATE"] = [("T", last, n, qt) for n in range(1, len(t_rounds(layer(last)))) for qt in range(QT)]
        keys["AT"] = [("AT", last)]
        keys["OUT"] = [("OUT", last)]
    if s == -1:
        keys["NORM"] = [("NORM", 0)]
        keys["VIP"] = [("VIP", 0)]
    if following is not None:
        keys["V"] = [("V", following, n) for n in range(len(v_parts(layer(following))))]
        keys["M"] = [("M", following)]
    if now is not None:
        keys["EARLY"] = [("T", now, 0, qt) for qt in range(QT)]
    for kind in sorted(keys, key=lambda kind: kind not in LONG):
        for place, key in zip(PLACES[regime(s)][kind], keys[kind]):
            at[place].append(key)
    return at


IP_NORMS, IP_ROOT, IP_LOGITS, IP_EXP, IP_WEIGHTS = 5, 5, 6, 8, 9


FIRST, LAST = -3, SLOTS


def hops_at(step):
    s = step // H
    return hops(s)[step % H] if FIRST <= s <= LAST else []


def hop_banks(s):
    return [5] if 0 <= s < B else [5, 6]


def score_banks(s):
    return [2, 3, 4] if s < 0 else [2, 3] if s < B else [2, 3, 7]


POOL_HEADS = 2


def steered_by_pool(n):
    return B * H <= n < 2 * B * H and n % POOL_HEADS == POOL_HEADS - 1


def steered_before(n, by_pool):
    pool = (n - B * H) // POOL_HEADS
    return pool if by_pool else n - B * H - pool


class Plan:

    def __init__(self):
        self.hop, n, used = {}, 0, {5: 0, 6: 0}
        for s in range(FIRST, LAST + 1):
            for pos in hops(s):
                for key in pos:
                    bank = hop_banks(s)[n % len(hop_banks(s))]
                    self.hop[key] = (n, bank, used[bank])
                    used[bank] += 1
                    n += 1
        on6 = [(n, k, used) for k, (n, bank, used) in self.hop.items() if bank == 6]
        start = self.hop[("K", 3)][0]
        self.hops_on_6_before_text = sum(1 for n, _, _ in on6 if n < start)
        self.first_on_6_after_text = min((n, k) for n, k, _ in on6 if n > start)[1]
        self.unit, last, n = {}, {}, 0
        for a in range(SLOTS):
            for j in range(QUADS):
                for u in range(4):
                    banks = score_banks(a - 2 + (j + 2) // QUADS)
                    bank = banks[n % len(banks)]
                    self.unit[(a, j, u)] = (n, bank, last.get(bank))
                    last[bank] = n
                    n += 1
        self.st = {}
        for n in range(SLOTS * H):
            self.st[n] = (n % 2, n - 2 if n >= 2 else None)
        order = []
        for n in range(SLOTS * H + 1):
            if n < SLOTS * H and not steered_by_pool(n):
                order.append(n)
            if steered_by_pool(n - 1):
                order.append(n - 1)
        self.exps = {n: i + 1 for i, n in enumerate(order)}
        self.sums, n = {}, 0
        for s in range(B, LAST + 1):
            for key in (key for pos in hops(s) for key in pos):
                if key[0] == "T" and layer(key[1]) > 0 and key[2:] != (len(t_rounds(layer(key[1]))) - 1, QT - 1):
                    n += 1
                    self.sums[key] = n
        self.split, n = {}, 0
        for s in range(FIRST, LAST + 1):
            for pos in hops(s):
                for key in pos:
                    if key[0] in ("K", "Q"):
                        self.split[key] = n
                        n += 1


def program(nc, t):
    plan = Plan()
    with ExitStack() as ctx:
        def sb(name, shape, dt=F32):
            return ctx.enter_context(nc.sbuf_tensor(name, shape, dt))

        def sem(name):
            return ctx.enter_context(nc.semaphore(name))

        bank = [ctx.enter_context(nc.psum_tensor(f"bank{i}", [P, 512], F32)) for i in range(8)]

        xT = sb("xT", [HALF, 2, B * S])
        ctxT = sb("ctxT", [P, 2, B * T])
        text = sb("text", [P, B * KT, E])
        wq = sb("wq", [HALF, NL, 2, C])
        wo = sb("wo", [HALF, NL, 2, C])
        bo = sb("bo", [HALF, NL, 2])
        wk = [sb(f"wk{l}", [P, len(SEGS[l]), 2, C]) for l in range(NL)]
        wv = [sb(f"wv{l}", [P, len(SEGS[l]), 2, C]) for l in range(NL)]
        spatial = sb("spatial", [P, QT])
        segmask = sb("segmask", [P, 3, KT, 4])
        ident = sb("ident", [P, P])
        identb = sb("identb", [P, P], BF16)
        ones = sb("ones", [P, P])
        kstack = sb("kstack", [P, 4, NS, T], BF16)
        qstack = sb("qstack", [P, 4, NS, S], BF16)
        ksplit = sb("ksplit", [HALF, 2, 3, T], BF16)
        qsplit = sb("qsplit", [HALF, 2, 3, S], BF16)
        rest = sb("rest", [HALF, 2, T])
        negmax = sb("negmax", [P, 2, QT, 4 * H])
        maxrest = sb("maxrest", [P, QT, 4 * H])
        maxsplit = sb("maxsplit", [P, QT, 3, 4 * H], BF16)
        maxT = sb("maxT", [120, 2, S], BF16)
        probs = sb("probs", [P, 8, KT, S])
        vals_wide = sb("vals_wide", [P, 2, KT, H, 64])
        vals_mid = sb("vals_mid", [P, 2, KT, H, 32])
        vals = [vals_wide[:, :, :, :, 0:32], vals_mid[:], vals_wide[:]]
        outT = sb("outT", [P, H // 2, S])
        rsum = sb("rsum", [P, QT, H, 4])
        scaled = sb("scaled", [P, QT, 32, D])
        attn = sb("attn", [P, QT, C])
        attnT = sb("attnT", [HALF, 2, S])
        s_ip = sb("s_ip", [P, 4, QT, H, NIP0])
        norm2 = sb("norm2", [P, 2, QT, H])
        dots = sb("dots", [P, QT, H, NIP0])
        ipsq = sb("ipsq", [P, 2, B, NIP0])
        ipn = sb("ipn", [P, 3, B, NIP0])
        v_ip = sb("v_ip", [P, 2, NIP0, C])
        ip_keys = sb("ip_keys", [P, 2, B * NIP0])
        nrm = sb("nrm", [P, 2, QT, H])
        fused = sb("fused", [P, 3, QT, H, NIP0])
        fsum = sb("fsum", [P, 2, QT, H])
        ipprod = sb("ipprod", [P, NIP0, C])
        ip_values = ipprod[0:B * NIP0, 0, :]
        qfull = sb("qfull", [HALF, 2, S])
        kfull = sb("kfull", [HALF, 2, NTEXT])
        textip = sb("textip", [NTEXT, T])
        pfull = sb("pfull", [P, 2, QT, NTEXT])
        fstat = sb("fstat", [P, 4, QT])
        pfullT = sb("pfullT", [NTEXT, S])
        steered = sb("steered", [P, 2, KT * S])
        semq = sb("semq", [P, 2, QT * T])
        semk = sb("semk", [P, 3, KT * S])

        ip_dram = nc.dram_tensor("ip_dram", [B, NIP0 * C], F32).ap()
        k_dram = nc.dram_tensor("k_dram", [SLOTS, 2, 3, HALF * T], BF16).ap()
        q_dram = nc.dram_tensor("q_dram", [SLOTS, 2, 3, HALF * S], BF16).ap()
        m_dram = nc.dram_tensor("m_dram", [SLOTS, 240, S], BF16).ap()

        loaded_x = sem("loaded_x")
        loaded_ctx = [sem(f"loaded_ctx{b}") for b in range(B)]
        loaded_text = sem("loaded_text")
        loaded_wk = [sem(f"loaded_wk{l}") for l in range(NL)]
        loaded_w = [sem(f"loaded_w{l}") for l in range(NL)]
        loaded_wo = sem("loaded_wo")
        loaded_const = sem("loaded_const")
        k_stored = sem("k_stored")
        q_stored = sem("q_stored")
        m_stored = sem("m_stored")
        k_loaded = [sem(f"k_loaded{i}") for i in range(4)]
        q_loaded = [sem(f"q_loaded{i}") for i in range(4)]
        m_loaded = [sem(f"m_loaded{i}") for i in range(4)]
        ip_stored = sem("ip_stored")
        v_ip_loaded = [sem("v_ip_loaded0"), sem("v_ip_loaded1")]
        out_stored = sem("out_stored")
        st_full = sem("st_full")
        st_steered = [sem("dve_steered"), sem("pool_steered")]
        pool_copied = sem("pool_copied")
        probs_ready = sem("probs_ready")
        s_full = sem("s_full")
        s_free = sem("s_free")
        o_full = sem("o_full")
        outT_ready = sem("outT_ready")
        y_full = sem("y_full")
        y_free = sem("y_free")
        hop_full = sem("hop_full")
        hop_taken = {5: sem("hop5_taken"), 6: sem("hop6_taken")}
        high_ready = sem("high_ready")
        rest_ready = sem("rest_ready")
        split_ready = sem("split_ready")
        maxsplit_ready = sem("maxsplit_ready")
        summed = sem("summed")
        attn_ready = sem("attn_ready")
        full_ready = sem("full_ready")
        textip_ready = sem("textip_ready")
        bias_ready = sem("bias_ready")
        pfull_ready = sem("pfull_ready")
        norm_ready = sem("norm_ready")
        root_ready = sem("root_ready")
        fused_ready = sem("fused_ready")
        weights_ready = sem("weights_ready")
        fexp_ready = sem("fexp_ready")
        text_masked = sem("text_masked")
        ipsq_ready = sem("ipsq_ready")
        vals_zeroed = sem("vals_zeroed")
        vals_marked = sem("vals_marked")
        ones_ready = sem("ones_ready")
        dve_step = sem("dve_step")
        pool_step = sem("pool_step")
        block = ctx.enter_context(nc.Block())

        def heads_of(unit):
            return unit // 2, unit % 2

        def scores_left(eng, n):
            if steered_by_pool(n):
                eng.wait_ge(pool_copied, steered_before(n, True) + 1)
            else:
                eng.wait_ge(probs_ready, plan.exps[n])

        def full_of(key):
            return plan.hop[key][0] + 1

        def hop_view(key):
            return bank[plan.hop[key][1]]

        def tr_view(l, key, units):
            r = HROWS[l]
            return hop_view(key)[:, 0:len(units) * P].rearrange("p (h r) -> p h r", r=r)

        def taken(eng, key):
            _, b, before = plan.hop[key]
            eng.wait_ge(hop_taken[b], before + 1)

        def softmaxes(key):
            _, s, rnd, qt = key
            g = 1 if layer(s) == 0 else len(SEGS[layer(s)])
            heads = len(t_rounds(layer(s))[rnd]) * P // HROWS[layer(s)]
            return scaled[:, qt, 0:heads * g].rearrange("p (h g) d -> p h g d", g=g)

        def last_values_hop(s):
            return ("V", s, len(v_parts(layer(s))) - 1)

        def st_count(s, h):
            return s * H + h + 1

        def quad_heads(j):
            return range(4 * j, 4 * j + 4)

        def k_dmas(s):
            return 6 if s < B or PATTERN[layer(s)] != PATTERN[layer(s) - 1] else 4

        def k_loaded_count(s):
            return 16 * sum(k_dmas(x) for x in range(batch(s), s + 1, B))

        @block.sync
        def _(sp):
            def load(dst, name, done):
                sp.dma_start(dst, t[name]).then_inc(done, 16)

            load(wk[0][:], "wk0", loaded_wk[0])
            sp.dma_start(ctxT[:, :, 0:T], t["ctxT"][:, :, 0:T]).then_inc(loaded_ctx[0], 16)
            load(wq[:], "wq", loaded_x)
            load(xT[:], "xT", loaded_x)

            def load_later(s):
                if s == FIRST:
                    for b in range(1, B):
                        sp.dma_start(ctxT[:, :, b * T:(b + 1) * T], t["ctxT"][:, :, b * T:(b + 1) * T])\
                            .then_inc(loaded_ctx[b], 16)
                    for name, dst in (("segmask", segmask), ("ident", ident), ("identb", identb),
                                      ("spatial", spatial), ("bo", bo)):
                        load(dst[:], name, loaded_const)
                if s == FIRST + 1:
                    load(wo[:], "wo", loaded_wo)
                    load(wv[0][:], "wv0", loaded_w[0])
                    load(text[:], "text", loaded_text)
                if 0 <= s < NL - 1:
                    load(wk[s + 1][:], f"wk{s + 1}", loaded_wk[s + 1])
                    load(wv[s + 1][:], f"wv{s + 1}", loaded_w[s + 1])

            def stack(kind, dst, src, done):
                high, middle, low = PARTS[kind]
                for half in range(2):
                    rows = src[half].rearrange("a (d x) -> a d x", d=D)
                    if kind == "K":
                        pieces = [src[half, 0:2].rearrange("a (d x) -> (a d) x", d=D).unsqueeze(0)
                                  .broadcast_to([2, 2 * D, NS * T]), rows[0:3:2]]
                    else:
                        pieces = [rows[high:high + 1].broadcast_to([2, D, NS * S]),
                                  rows[middle:middle + 1].broadcast_to([2, D, NS * S]), rows[0:2]]
                    row = 64 * half
                    for piece in pieces:
                        n = ROWS - 4 * D if piece is pieces[-1] else 4 * D // (len(pieces) - 1)
                        sp.dma_start(dst[row:row + n, :], piece).then_inc(done, 16)
                        row += n

            def keys_to_stack(k):
                if k >= B:
                    sp.wait_ge(st_full, st_count(k - B, H - 1))
                sp.wait_ge(split_ready, plan.split[("K", k)] + 1)
                sp.dma_start(k_dram[k].rearrange("h a (p t) -> p (h a) t", p=HALF),
                             ksplit[:].rearrange("p h a t -> p (h a) t")).then_inc(k_stored, 16)
                if k_dmas(k) == 6:
                    n = 3 * len(SEGS[layer(k)])
                    for half in range(2):
                        sp.dma_start(kstack[64 * half + ROWS:64 * half + ROWS + n, batch(k)]
                                     .rearrange("r s t -> r (s t)"),
                                     t[f"marks{PATTERN[layer(k)]}"]).then_inc(k_loaded[batch(k)], 16)
                sp.wait_ge(k_stored, 16 * (k + 1))
                stack("K", kstack[:, batch(k)].rearrange("r s t -> r (s t)"), k_dram[k], k_loaded[batch(k)])

            def queries_to_stack(k):
                sp.wait_ge(split_ready, plan.split[("Q", k)] + 1)
                sp.dma_start(q_dram[k].rearrange("h a (p t) -> p (h a) t", p=HALF),
                             qsplit[:].rearrange("p h a t -> p (h a) t")).then_inc(q_stored, 16)
                sp.wait_ge(q_stored, 16 * (k + 1))
                stack("Q", qstack[:, batch(k)].rearrange("r s t -> r (s t)"), q_dram[k], q_loaded[batch(k)])

            def maxima_to_stack(m):
                nblk = len(SEGS[layer(m)]) * 3 * H // 120
                taken(sp, ("M", m))
                sp.dma_start(m_dram[m, 0:nblk * 120].rearrange("(n p) q -> p n q", n=nblk),
                             maxT[:, 0:nblk, :]).then_inc(m_stored, 16)
                sp.wait_ge(m_stored, 16 * (m + 1))
                n = 3 * len(SEGS[layer(m)])
                for half in range(2):
                    sp.dma_start(qstack[64 * half + ROWS:64 * half + ROWS + n, batch(m)],
                                 m_dram[m, 0:n * H].rearrange("(r h s) q -> h r s q", h=2, s=NS)[half])\
                        .then_inc(m_loaded[batch(m)], 16)

            for s in range(FIRST, LAST):
                if s != FIRST + 1:
                    load_later(s)
                if s + 3 < SLOTS:
                    keys_to_stack(s + 3)
                if s < -1:
                    queries_to_stack(s + 3)
                if s == FIRST + 1:
                    load_later(s)
                if 0 <= s + 1 < SLOTS:
                    maxima_to_stack(s + 1)
                if s == -1:
                    taken(sp, ("VIP", 0))
                    sp.dma_start(ip_dram.rearrange("b (n c) -> (b n) c", n=NIP0), ip_values).then_inc(ip_stored, 16)
                    sp.wait_ge(ip_stored, 16)
                if 0 <= s + 1 < B:
                    if s >= 1:
                        sp.wait_ge(attn_ready, s)
                    sp.dma_start(v_ip[:, (s + 1) % 2].rearrange("p n c -> p (n c)"),
                                 ip_dram[s + 1:s + 2].broadcast_to([P, NIP0 * C])).then_inc(v_ip_loaded[(s + 1) % 2], 16)
                if s >= 1 and layer(s - 1) == NL - 1:
                    taken(sp, ("OUT", s - 1))
                    b = batch(s - 1)
                    sp.dma_start(t["out"][:, :, b * S:(b + 1) * S], xT[:, :, b * S:(b + 1) * S]).then_inc(out_stored, 16)
                if -1 <= s and s + 3 < SLOTS:
                    queries_to_stack(s + 3)
            taken(sp, ("OUT", SLOTS - 1))
            b = B - 1
            sp.dma_start(t["out"][:, :, b * S:(b + 1) * S], xT[:, :, b * S:(b + 1) * S]).then_inc(out_stored, 16)
            sp.wait_ge(out_stored, 16 * B)

        @block.tensor
        def _(pe):
            mm = nc.tensor.matmul

            def begin(key):
                n, b, before = plan.hop[key]
                if before:
                    pe.wait_ge(hop_taken[b], before)
                if key == plan.first_on_6_after_text:
                    pe.wait_ge(y_free, B * H)
                return bank[b]

            def scores_for_max(a, j, u):
                qt, half = heads_of(u)
                n, b, last = plan.unit[(a, j, u)]
                if j == 0 and u == 0:
                    pe.wait_ge(k_loaded[batch(a)], k_loaded_count(a))
                    pe.wait_ge(q_loaded[batch(a)], 96 * (layer(a) + 1))
                if last is not None:
                    pe.wait_ge(s_free, last + 1)
                elif b == 7:
                    pe.wait_ge(y_free, B * H)
                r0 = 64 * half
                out = bank[b]
                for i in range(2):
                    ins = mm(out[:, i * T:(i + 1) * T],
                             qstack[r0:r0 + ROWS, batch(a), 2 * j + i, qt * P:(qt + 1) * P],
                             kstack[r0:r0 + ROWS, batch(a), 2 * j + i, :],
                             start=True, stop=True)
                ins.then_inc(s_full, 1)

            def scores_for_exp(s, h):
                if h == 0:
                    pe.wait_ge(m_loaded[batch(s)], 32 * (layer(s) + 1))
                n = s * H + h
                b, last = plan.st[n]
                if last is not None:
                    scores_left(pe, last)
                r0, rows = 64 * (h % 2), ROWS + 3 * len(SEGS[layer(s)])
                out = bank[b]
                for c in range(KT):
                    ins = mm(out[:, c * S:(c + 1) * S],
                             kstack[r0:r0 + rows, batch(s), h // 2, c * P:(c + 1) * P],
                             qstack[r0:r0 + rows, batch(s), h // 2, :],
                             start=True, stop=True)
                ins.then_inc(st_full, 1)

            def values_product(s, j, part):
                l = layer(s)
                rows, buf = HROWS[l], vals[PATTERN[l]]
                if j == 0 and part == 0:
                    pe.wait_ge(vals_marked, 2 if l == 3 else 1)
                    taken(pe, last_values_hop(s))
                pe.wait_ge(probs_ready, max(plan.exps[s * H + h] for h in quad_heads(j)))
                n = s * QUADS + j
                if n and part == 0:
                    pe.wait_ge(outT_ready, n)
                if n == 0 and part == 0:
                    pe.wait_ge(s_free, max(i for i, b, _ in plan.unit.values() if b == 4) + 1)
                per = P // rows
                for c in ([part] if per == 4 else range(KT)):
                    for i in (range(4) if per == 4 else range(2 * part, 2 * part + 2)):
                        h, r = 4 * j + i, i % per
                        ins = mm(bank[4][r * rows:(r + 1) * rows, i // per * S:(i // per + 1) * S],
                                 buf[:, s % 2, c, h, :], probs[:, (s * H + h) % 8, c, :],
                                 start=(c == 0), stop=(c == KT - 1))
                if part == 1:
                    ins.then_inc(o_full, 1)

            def text_product(s, h):
                n = s * H + h
                if n >= 2:
                    pe.wait_ge(y_free, n - 1)
                elif n == 0:
                    pe.wait_ge(text_masked, 1)
                    pe.wait_ge(hop_taken[6], plan.hops_on_6_before_text)
                pe.wait_ge(probs_ready, plan.exps[n])
                out = bank[6 + n % 2]
                for qt in range(QT):
                    for c in range(KT):
                        ins = mm(out[:, qt * E:(qt + 1) * E], probs[:, n % 8, c, qt * P:(qt + 1) * P],
                                 text[:, KT * batch(s) + c, :], start=(c == 0), stop=(c == KT - 1))
                ins.then_inc(y_full, 1)

            def project(out, w, src, cols, halves):
                for half in halves:
                    for k in range(2):
                        ins = mm(out[0:HALF, half * cols:(half + 1) * cols], w[:, k, half * HALF:(half + 1) * HALF],
                                 src[:, k, :], start=(k == 0), stop=(k == 1))
                return ins

            def long_hop(key, part):
                kind, s = key[0], key[1]
                l, b = layer(s), batch(s)
                out = bank[plan.hop[key][1]]
                if kind == "K":
                    if part == 0:
                        if l == 0:
                            pe.wait_ge(loaded_ctx[b], 16)
                        if b == 0:
                            pe.wait_ge(loaded_wk[l], 16)
                        begin(key)
                    for g, (a, z) in enumerate(SEGS[l]):
                        for e in range(2):
                            ins = mm(out[0:HALF, part * T + a:part * T + z],
                                     wk[l][:, g, e, part * HALF:(part + 1) * HALF],
                                     ctxT[:, e, b * T + a:b * T + z], start=(e == 0), stop=(e == 1))
                elif kind == "Q":
                    if part == 0:
                        if s == 0:
                            pe.wait_ge(loaded_x, 16 * 2)
                        if s >= B:
                            taken(pe, ("OUT", s - B))
                        begin(key)
                    ins = project(out, wq[:, l], xT[:, :, b * S:(b + 1) * S], S, [part])
                elif kind == "OUT":
                    if part == 0:
                        if s == 0:
                            pe.wait_ge(loaded_wo, 16)
                        taken(pe, ("AT", s))
                        begin(key)
                    ins = project(out, wo[:, l], attnT[:], S, [part])
                elif kind == "V":
                    if part == 0:
                        if b == 0:
                            pe.wait_ge(loaded_w[l], 16)
                        begin(key)
                    pairs = list(enumerate(v_parts(l)[key[2]]))
                    cut = (len(pairs) + 1) // 2
                    for i, (c, g) in pairs[cut:] if part else pairs[:cut]:
                        for e in range(2):
                            ins = mm(out[:, i * C:(i + 1) * C], ctxT[:, e, b * T + c * P:b * T + (c + 1) * P],
                                     wv[l][:, g, e, :], start=(e == 0), stop=(e == 1))
                    if l == 0 and part == 1:
                        for c in range(KT):
                            for e in range(2):
                                ins = mm(out[:, 2 * C + c * NIP0:2 * C + (c + 1) * NIP0],
                                         ctxT[:, e, b * T + c * P:b * T + (c + 1) * P],
                                         ctxT[:, e, (b + 1) * T - NIP0:(b + 1) * T], start=(e == 0), stop=(e == 1))
                if part == 1:
                    ins.then_inc(hop_full, 1)

            def hop(key):
                kind, s = key[0], key[1]
                l, b = layer(s), batch(s)
                if kind == "NORM":
                    pe.wait_ge(ones_ready, 1)
                    pe.wait_ge(ipsq_ready, 1)
                    out = begin(key)
                    for e in range(2):
                        ins = mm(out[:, 0:B * NIP0], ones[:], ipsq[:, e].rearrange("p b n -> p (b n)"),
                                 start=(e == 0), stop=(e == 1))
                elif kind == "M":
                    if s == 0:
                        pe.wait_ge(loaded_const, 16 * CONSTANTS)
                    pe.wait_ge(maxsplit_ready, s + 1)
                    out = begin(key)[:].bitcast(BF16)
                    n = 3 * len(SEGS[l]) * H
                    for qt in range(QT):
                        flat = maxsplit[:, qt].rearrange("p a n -> p (a n)")
                        for k in range(n // 120):
                            ins = nc.tensor.transpose(out[0:120, k * S + qt * P:k * S + (qt + 1) * P],
                                                      flat[:, k * 120:(k + 1) * 120], identb[:])
                elif kind == "T":
                    _, _, n, qt = key
                    units = t_rounds(l)[n]
                    per = 4 * HROWS[l] // P
                    pe.wait_ge(outT_ready, s * QUADS + units[-1] // per + 1)
                    out = begin(key)
                    for i, u in enumerate(units):
                        ins = nc.tensor.transpose(out[:, i * P:(i + 1) * P], outT[:, u, qt * P:(qt + 1) * P],
                                                  ident[:])
                elif kind == "AT":
                    pe.wait_ge(attn_ready, s + 1)
                    out = begin(key)
                    for half in range(2):
                        for qt in range(QT):
                            ins = nc.tensor.transpose(out[0:HALF, half * S + qt * P:half * S + (qt + 1) * P],
                                                      attn[:, qt, half * HALF:(half + 1) * HALF], ident[:])
                elif kind == "VIP":
                    pe.wait_ge(loaded_w[0], 16)
                    out = begin(key)
                    for e in range(2):
                        ins = mm(out[0:B * NIP0, 0:C], ip_keys[:, e, :], wv[0][:, 1, e, :], start=(e == 0), stop=(e == 1))
                elif kind == "FULL":
                    out = begin(key)
                    for e in range(2):
                        mm(out[0:NTEXT, 0:T - NTEXT], ctxT[:, e, b * T:b * T + NTEXT],
                           ctxT[:, e, b * T + NTEXT:(b + 1) * T], start=(e == 0), stop=(e == 1))
                    pe.wait_ge(full_ready, 2 * (b + 1))
                    for qt in range(QT):
                        for k in range(2):
                            ins = mm(out[:, 256 + qt * NTEXT:256 + (qt + 1) * NTEXT], qfull[:, k, qt * P:(qt + 1) * P],
                                     kfull[:, k, :], start=(k == 0), stop=(k == 1))
                elif kind == "PT":
                    pe.wait_ge(pfull_ready, b + 1)
                    out = begin(key)
                    for qt in range(QT):
                        ins = nc.tensor.transpose(out[0:NTEXT, qt * P:(qt + 1) * P], pfull[:, 1, qt, :], ident[:])
                elif kind == "SEM":
                    taken(pe, ("PT", s))
                    out = begin(key)
                    for qt in range(QT):
                        ins = mm(out[:, qt * T:(qt + 1) * T], pfullT[:, qt * P:(qt + 1) * P], textip[:],
                                 start=True, stop=True)
                elif kind == "SEMT":
                    out = begin(key)
                    for c in range(KT):
                        ins = mm(out[:, c * S:(c + 1) * S], textip[:, c * P:(c + 1) * P], pfullT[:],
                                 start=True, stop=True)
                ins.then_inc(hop_full, 1)

            for s in range(FIRST, LAST + 1):
                exp = 0 <= s < SLOTS
                at = hops(s)
                for h in range(H):
                    j, u = divmod(h, 4)
                    a, k = score_quad(s, j)
                    if exp:
                        scores_for_exp(s, h)
                    if 0 <= a < SLOTS:
                        scores_for_max(a, k, u)
                    done = behind(s, h)
                    if done:
                        if u - values_step(s) in (0, 1):
                            values_product(done[0], done[1] // 4, u - values_step(s))
                        if layer(done[0]) == 0:
                            for key in at[h][:-1]:
                                hop(key)
                            at[h] = at[h][-1:]
                            text_product(*done)
                    for key in at[h]:
                        if key[0] in LONG:
                            long_hop(key, 1)
                        else:
                            hop(key)
                    for key in at[h + 1] if h + 1 < H else []:
                        if key[0] in LONG:
                            long_hop(key, 0)
                if s in (B - 1, SLOTS - 1):
                    for part in range(2):
                        values_product(s, QUADS - 1, part)
                    if layer(s) == 0:
                        for h in quad_heads(QUADS - 1):
                            text_product(s, h)

        @block.scalar
        def _(act):
            def copy(out, in_, scale=None):
                if scale is None:
                    return nc.scalar.activation(out, in_, ACT.Copy)
                return nc.scalar.activation(out, in_, ACT.Copy, scale=scale)

            def exponentials(s, h):
                n = s * H + h
                source = bank[plan.st[n][0]][:]
                if layer(s) == 1:
                    by_pool = steered_by_pool(n)
                    act.wait_ge(st_steered[by_pool], steered_before(n, by_pool) + 1)
                    if by_pool:
                        source = steered[:, n // POOL_HEADS % 2]
                else:
                    act.wait_ge(st_full, n + 1)
                if n >= 8 and h % 4 == 0:
                    q = s * QUADS + h // 4
                    act.wait_ge(o_full, q - 1)
                    if q - 1 <= B * QUADS:
                        act.wait_ge(y_full, 4 * (q - 1))
                    elif q - 2 < B * QUADS:
                        act.wait_ge(y_full, B * H)
                nc.scalar.activation(probs[:, n % 8].rearrange("p c q -> p (c q)"), source, ACT.Exp,
                                     scale=SCALE).then_inc(probs_ready, 1)

            def copy_for_pool(s, h):
                n = s * H + h
                act.wait_ge(st_full, n + 1)
                if n - 2 * POOL_HEADS >= B * H:
                    act.wait_ge(probs_ready, plan.exps[n - 2 * POOL_HEADS])
                copy(steered[:, n // POOL_HEADS % 2], bank[plan.st[n][0]][:]).then_inc(pool_copied, 1)

            def take_out(s, j):
                l = layer(s)
                n = s * QUADS + j
                per = 4 * HROWS[l] // P
                if j == 0 and s >= 1:
                    last = t_rounds(layer(s - 1))
                    act.wait_ge(hop_full, full_of(("T", s - 1, len(last) - 1, QT - 1)))
                act.wait_ge(o_full, n + 1)
                copy(outT[:, per * j:per * (j + 1), :],
                     bank[4][:, 0:per * S].rearrange("p (u q) -> p u q", u=per)).then_inc(outT_ready, 1)

            def square_norm(s, h):
                n = s * H + h
                if h == 0 and s >= 2:
                    act.wait_ge(attn_ready, s - 1)
                act.wait_ge(y_full, n + 1)
                for qt in range(QT):
                    y = bank[6 + n % 2][:, qt * E:(qt + 1) * E]
                    ins = nc.scalar.activation(y, y, ACT.Square, accum_out=norm2[:, s % 2, qt, h:h + 1])
                ins.then_inc(y_free, 1)

            def image_roots(s):
                act.wait_ge(norm_ready, s + 1)
                nc.scalar.activation(nrm[:, 1], nrm[:, 0], ACT.Sqrt).then_inc(root_ready, 1)

            def image_exponentials(s):
                act.wait_ge(fused_ready, s + 1)
                nc.scalar.activation(fused[:, 2], fused[:, 1], ACT.Exp, scale=SCALE).then_inc(fexp_ready, 1)

            def hop(key):
                kind, s = key[0], key[1]
                l, b = layer(s), batch(s)
                n, hb, _ = plan.hop[key]
                src = bank[hb]
                if kind == "NORM":
                    taken(act, key)
                    nc.scalar.activation(ipn[:, 1], ipn[:, 0], ACT.Sqrt).then_inc(root_ready, 1)
                elif kind in ("K", "Q"):
                    act.wait_ge(hop_full, n + 1)
                    dst, stored = (ksplit, k_stored) if kind == "K" else (qsplit, q_stored)
                    if s:
                        act.wait_ge(stored, 16 * s)
                    if l == 1:
                        if kind == "K":
                            if b:
                                act.wait_ge(hop_full, full_of(("FULL", s - 1)))
                            copy(kfull[:], src[0:HALF].rearrange("p (h t) -> p h t", h=2)[:, :, 0:NTEXT])\
                                .then_inc(full_ready, 1)
                        else:
                            copy(qfull[:].rearrange("p h q -> p (h q)"), src[0:HALF]).then_inc(full_ready, 1)
                    copy(dst[:, :, PARTS[kind][0]], src[0:HALF].rearrange("p (h t) -> p h t", h=2)).then_inc(high_ready, 1)
                elif kind == "M":
                    act.wait_ge(hop_full, n + 1)
                    if s:
                        act.wait_ge(m_stored, 16 * s)
                    nblk = 3 * len(SEGS[l]) * H // 120
                    copy(maxT[:, 0:nblk].rearrange("p n q -> p (n q)"), src[:].bitcast(BF16)[0:120, 0:nblk * S])\
                        .then_inc(hop_taken[hb], 1)
                elif kind == "AT":
                    act.wait_ge(hop_full, n + 1)
                    copy(attnT[:].rearrange("p h q -> p (h q)"), src[0:HALF]).then_inc(hop_taken[hb], 1)
                elif kind == "V":
                    act.wait_ge(hop_full, n + 1)
                    buf = vals[PATTERN[l]]
                    if key[2] == 0:
                        act.wait_ge(vals_zeroed, 3 if l == 3 else 2)
                        if s >= 2:
                            act.wait_ge(o_full, (s - 1) * QUADS)
                    for i, (c, g) in enumerate(v_parts(l)[key[2]]):
                        ins = copy(buf[:, s % 2, c, :, 9 * g:9 * g + D],
                                   src[:, i * C:(i + 1) * C].rearrange("p (h d) -> p h d", h=H),
                                   segmask[:, PATTERN[l], c, g:g + 1])
                    if l == 0:
                        for c in range(KT):
                            ins = copy(buf[:, s % 2, c, :, 9:9 + NIP0],
                                       src[:, 2 * C + c * NIP0:2 * C + (c + 1) * NIP0].unsqueeze(1)
                                       .broadcast_to([P, H, NIP0]), segmask[:, 0, c, 0:1])
                    ins.then_inc(hop_taken[hb], 1)
                elif kind == "VIP":
                    act.wait_ge(hop_full, n + 1)
                    copy(ip_values, src[0:B * NIP0, 0:C]).then_inc(hop_taken[hb], 1)
                elif kind == "FULL":
                    act.wait_ge(hop_full, n + 1)
                    if b:
                        act.wait_ge(hop_full, full_of(("SEMT", s - 1)))
                    copy(textip[:, NTEXT:T], src[0:NTEXT, 0:T - NTEXT]).then_inc(textip_ready, 1)
                    act.wait_ge(bias_ready, b + 1)
                    for qt in range(QT):
                        ins = nc.scalar.activation(pfull[:, 0, qt, :], src[:, 256 + qt * NTEXT:256 + (qt + 1) * NTEXT],
                                                   ACT.Exp, bias=fstat[:, 1, qt:qt + 1], scale=SCALE,
                                                   accum_out=fstat[:, 2, qt:qt + 1])
                    ins.then_inc(hop_taken[hb], 1)
                elif kind == "PT":
                    act.wait_ge(hop_full, n + 1)
                    copy(pfullT[:], src[0:NTEXT, 0:S]).then_inc(hop_taken[hb], 1)
                elif kind == "SEM":
                    act.wait_ge(hop_full, n + 1)
                    if b >= 2:
                        act.wait_ge(s_free, (s - 1) * 4 * QUADS)
                    copy(semq[:, s % 2], src[:], 0.5).then_inc(hop_taken[hb], 1)
                elif kind == "SEMT":
                    act.wait_ge(hop_full, n + 1)
                    if b == 3:
                        for i in range(2):
                            act.wait_ge(st_steered[i], steered_before((s - 2) * H, bool(i)))
                    copy(semk[:, s % 3], src[:], 0.5).then_inc(hop_taken[hb], 1)

            def middle_part(key):
                parts = (ksplit if key[0] == "K" else qsplit)[:].rearrange("p h a t -> p a h t")
                taken(act, key)
                copy(parts[:, PARTS[key[0]][1]], rest[:]).then_inc(rest_ready, 1)

            for s in range(FIRST, LAST + 1):
                exp = 0 <= s < SLOTS
                if s == -2:
                    act.wait_ge(loaded_const, 16 * CONSTANTS)
                for h, keys in enumerate(hops(s)):
                    u = h % 4
                    n = s * H + h
                    if steered_by_pool(n):
                        copy_for_pool(s, h)
                    elif exp:
                        exponentials(s, h)
                    if steered_by_pool(n - 1):
                        exponentials((n - 1) // H, (n - 1) % H)
                    done = behind(s, h)
                    if done:
                        if u == values_step(s) + 1:
                            take_out(done[0], done[1] // 4)
                        if layer(done[0]) == 0:
                            for key in keys[:-1]:
                                hop(key)
                            keys = keys[-1:]
                            square_norm(*done)
                    for key in hops_at(s * H + h - 1):
                        if key[0] in ("K", "Q"):
                            middle_part(key)
                    if h == IP_ROOT and s >= 1 and layer(s - 1) == 0:
                        image_roots(s - 1)
                    if h == IP_EXP and s >= 1 and layer(s - 1) == 0:
                        image_exponentials(s - 1)
                    for key in keys:
                        hop(key)
                if s in (B - 1, SLOTS - 1):
                    take_out(s, QUADS - 1)
                    if layer(s) == 0:
                        for h in quad_heads(QUADS - 1):
                            square_norm(s, h)

        @block.vector
        def _(dve):
            steps = [0]
            marks = {}

            def mark(ins, name):
                steps[0] += 1
                ins.then_inc(dve_step, 1)
                marks[name] = steps[0]

            def marked(name):
                dve.wait_ge(dve_step, marks[name])

            def link(ins):
                mark(ins, "link")
                marked("link")

            tt, ts, stt = nc.vector.tensor_tensor, nc.vector.tensor_scalar, nc.vector.scalar_tensor_tensor

            def maxima(a, j, u):
                qt, half = heads_of(u)
                n, b, _ = plan.unit[(a, j, u)]
                l = layer(a)
                dve.wait_ge(s_full, n + 1)
                src = bank[b][:].rearrange("p (s t) -> p s t", s=2)
                dst = negmax[:, a % 2, qt, 0:len(SEGS[l]) * H]\
                    .rearrange("p (g e s) -> p s g e", g=len(SEGS[l]), e=2)[:, 2 * j:2 * j + 2, :, half]

                if l == 1 and j == 0 and u == 0:
                    taken(dve, ("SEM", a))

                def take(g, z):
                    lo, hi = SEGS[l][g][0], SEGS[l][z - 1][1]
                    return nc.vector.tensor_reduce(
                        dst[:, :, g:z], src[:, :, lo:hi].rearrange("p s (g k) -> p s g k", g=z - g),
                        AX.X, ALU.max, negate=True)
                if l == 0:
                    nc.vector.tensor_copy(
                        s_ip[:, batch(a), qt].rearrange("p (s e) n -> p s e n", e=2)[:, 2 * j:2 * j + 2, half, :],
                        src[:, :, T - NIP0:T])
                runs = {0: [(0, 1), (1, 2)], 1: [(0, 1)], 2: [(0, 1), (1, 2)], 3: [(0, 1), (1, 3), (3, 4)]}[l]
                for g, z in runs:
                    ins = take(g, z)
                if l == 1:
                    lo = SEGS[1][1][0]
                    for i in range(2):
                        x = src[:, i, lo:T]
                        ins = nc.vector.tensor_tensor_reduce(
                            out=x, in0=x, in1=semq[:, a % 2, qt * T + lo:(qt + 1) * T], scale=-1.0,
                            scalar=3.0e38, op0=ALU.add, op1=ALU.min, accum_out=dst[:, i, 1:2])
                ins.then_inc(s_free, 1)

            def steer(s, h):
                n = s * H + h
                if h == 0:
                    taken(dve, ("SEMT", s))
                dve.wait_ge(st_full, n + 1)
                scores = bank[plan.st[n][0]][:]
                tt(scores, scores, semk[:, s % 3], ALU.add).then_inc(st_steered[0], 1)

            def wide(x):
                return x.unsqueeze(3).broadcast_to([P, QT, H, NIP0])

            def image_norms(s):
                dve.wait_ge(y_free, (s + 1) * H)
                taken(dve, ("T", s, len(t_rounds(0)) - 1, QT - 1))
                link(tt(nrm[:, 0], norm2[:, s % 2], rsum[:, :, :, 0], ALU.mult))
                link(tt(nrm[:, 1], nrm[:, 0], rsum[:, :, :, 0], ALU.mult))
                nc.vector.tensor_scalar_max(nrm[:, 0], nrm[:, 1], EPS2).then_inc(norm_ready, 1)

            def image_logits(s):
                flat = fused[:].rearrange("p i q h n -> p i (q h) n")
                line = fused[:].rearrange("p i q h n -> p i (q h n)")
                dve.wait_ge(root_ready, s + 2)
                link(nc.vector.reciprocal(nrm[:, 0], nrm[:, 1]))
                link(tt(fused[:, 0], dots[:], wide(nrm[:, 0]), ALU.mult))
                link(tt(flat[:, 1], flat[:, 0], ipn[:, 2, batch(s)].unsqueeze(1).broadcast_to([P, QT * H, NIP0]),
                        ALU.mult))
                link(stt(line[:, 0], line[:, 1], 0.5 / SCALE,
                         s_ip[:, batch(s)].rearrange("p q h n -> p (q h n)"), ALU.mult, ALU.add))
                link(nc.vector.tensor_reduce(fsum[:, 0], fused[:, 0], AX.X, ALU.max))
                tt(fused[:, 1], fused[:, 0], wide(fsum[:, 0]), ALU.subtract).then_inc(fused_ready, 1)

            def image_weights(s):
                dve.wait_ge(fexp_ready, s + 1)
                link(nc.vector.tensor_reduce(fsum[:, 0], fused[:, 2], AX.X, ALU.add))
                link(nc.vector.reciprocal(fsum[:, 1], fsum[:, 0]))
                link(tt(fsum[:, 0], fsum[:, 1], spatial[:].unsqueeze(2).broadcast_to([P, QT, H]), ALU.mult))
                tt(fused[:, 0], fused[:, 2], wide(fsum[:, 0]), ALU.mult).then_inc(weights_ready, 1)

            def hop(key):
                kind, s = key[0], key[1]
                l, b = layer(s), batch(s)
                n, hb, before = plan.hop[key]
                src = bank[hb]
                if kind == "NORM":
                    dve.wait_ge(hop_full, n + 1)
                    nc.vector.tensor_scalar_max(ipn[:, 0].rearrange("p b n -> p (b n)"), src[:, 0:B * NIP0], EPS2)\
                        .then_inc(hop_taken[hb], 1)
                    dve.wait_ge(root_ready, 1)
                    link(nc.vector.reciprocal(ipn[:, 2], ipn[:, 1]))
                elif kind in ("K", "Q"):
                    i = plan.split[key]
                    dve.wait_ge(high_ready, i + 1)
                    if i:
                        dve.wait_ge(split_ready, i)
                    parts = (ksplit if kind == "K" else qsplit)[:].rearrange("p h a t -> p a h t")
                    left = rest[:]
                    tt(left, src[0:HALF].rearrange("p (h t) -> p h t", h=2), parts[:, PARTS[kind][0]], ALU.subtract).then_inc(hop_taken[hb], 1)
                elif kind == "OUT":
                    dve.wait_ge(hop_full, n + 1)
                    for half in range(2):
                        x = xT[:, half, b * S:(b + 1) * S]
                        ins = stt(x, src[0:HALF, half * S:(half + 1) * S], bo[:, l, half:half + 1], x, ALU.add, ALU.add)
                    ins.then_inc(hop_taken[hb], 1)
                elif kind == "FULL":
                    dve.wait_ge(textip_ready, b + 1)
                    link(nc.vector.tensor_reduce(fstat[:, 0], src[:, 256:256 + QT * NTEXT]
                                                 .rearrange("p (q t) -> p q t", q=QT), AX.X, ALU.max, negate=True))
                    ts(fstat[:, 1], fstat[:, 0], SCALE, None, ALU.mult).then_inc(bias_ready, 1)
                    taken(dve, key)
                    link(nc.vector.reciprocal(fstat[:, 3], fstat[:, 2]))
                    for qt in range(QT):
                        ins = ts(pfull[:, 1, qt], pfull[:, 0, qt], fstat[:, 3, qt:qt + 1], None, ALU.mult)
                    ins.then_inc(pfull_ready, 1)

            def normalise(key, stage):
                _, s, rnd, qt = key
                l = layer(s)
                n, hb, _ = plan.hop[key]
                units = t_rounds(l)[rnd]
                per = P // HROWS[l]
                h0, h1 = units[0] * per, (units[-1] + 1) * per
                nh, g = h1 - h0, 1 if l == 0 else len(SEGS[l])
                view = tr_view(l, key, units)
                parts = view[:, :, 0:9 * g].rearrange("p h (g k) -> p h g k", k=9)
                sums = softmaxes(key)
                if stage == 0:
                    dve.wait_ge(hop_full, n + 1)
                    mark(nc.vector.reciprocal(rsum[:, qt, h0:h1, 0:g], parts[:, :, :, D]), key)
                elif stage == 1:
                    marked(key)
                    if rnd == 0 and qt == 0 and s:
                        dve.wait_ge(hop_full, full_of(("AT", s - 1)))
                    if l == 0:
                        tt(attn[:, qt, h0 * D:h1 * D].rearrange("p (h d) -> p h d", h=nh), view[:, :, 0:D],
                           rsum[:, qt, h0:h1, 0:1].broadcast_to([P, nh, D]), ALU.mult)
                        tt(dots[:, qt, h0:h1], view[:, :, 9:9 + NIP0],
                           rsum[:, qt, h0:h1, 0:1].broadcast_to([P, nh, NIP0]), ALU.mult).then_inc(hop_taken[hb], 1)
                        return
                    if rnd:
                        dve.wait_ge(summed, plan.sums[("T", s, rnd - 1, qt)])
                    tt(sums, parts[:, :, :, 0:D],
                       rsum[:, qt, h0:h1, 0:g].unsqueeze(3).broadcast_to([P, nh, g, D]), ALU.mult)\
                        .then_inc(hop_taken[hb], 1)

            def split_maxima(a, stage):
                n = len(SEGS[layer(a)]) * H
                src, left = negmax[:, a % 2, :, 0:n], maxrest[:, :, 0:n]
                flat = maxsplit[:].rearrange("p q a n -> p q (a n)")
                part = [flat[:, :, p * n:(p + 1) * n] for p in range(3)]
                if stage == 0:
                    dve.wait_ge(s_free, (a + 1) * 4 * QUADS)
                    if a:
                        dve.wait_ge(hop_full, full_of(("M", a - 1)))
                    mark(nc.vector.tensor_copy(part[0], src), "split")
                    return
                marked("split")
                if stage == 1:
                    mark(tt(left, src, part[0], ALU.subtract), "split")
                elif stage == 2:
                    mark(nc.vector.tensor_copy(part[1], left), "split")
                else:
                    tt(part[2], left, part[1], ALU.subtract).then_inc(maxsplit_ready, 1)

            dve.wait_ge(ones_ready, 1)

            def mark_segments(zeroed, patterns):
                dve.wait_ge(vals_zeroed, zeroed)
                for pattern, segs in patterns:
                    for c in range(KT):
                        for g in range(segs):
                            ins = ts(vals[pattern][:, :, c, :, 9 * g + D],
                                     ones[:, 0:2 * H].rearrange("p (i h) -> p i h", i=2),
                                     segmask[:, pattern, c, g:g + 1], None, ALU.mult)
                ins.then_inc(vals_marked, 1)

            for b in range(B):
                dve.wait_ge(loaded_ctx[b], 16)
            ip = ctxT[:].rearrange("p e (b t) -> p e b t", b=B)[:, :, :, T - NIP0:T]
            for e in range(2):
                nc.vector.tensor_copy(ip_keys[:, e].rearrange("p (b n) -> p b n", b=B), ip[:, e])
                ins = tt(ipsq[:, e], ip[:, e], ip[:, e], ALU.mult)
            ins.then_inc(ipsq_ready, 1)
            for s in range(FIRST, LAST + 1):
                at = hops(s)
                if s == -2:
                    dve.wait_ge(loaded_const, 16 * CONSTANTS)
                    mark_segments(2, ((0, 1), (1, 2)))
                if s == 0:
                    dve.wait_ge(loaded_text, 16)
                    odd = text[:].rearrange("p (b c) e -> p c b e", c=KT)[:, 1]
                    ts(odd, odd, segmask[:, 0, 1, 0:1], None, ALU.mult).then_inc(text_masked, 1)
                for h, keys in enumerate(at):
                    j, u = divmod(h, 4)
                    a, k = score_quad(s, j)
                    if 0 <= s < SLOTS and layer(s) == 1 and not steered_by_pool(s * H + h):
                        steer(s, h)
                    if 0 <= a < SLOTS:
                        maxima(a, k, u)
                    for stage in (1, 0):
                        for key in hops_at(s * H + h - stage):
                            if key[0] == "T" and not 0 <= s * H + h - stage < B * H:
                                normalise(key, stage)
                    for key in keys:
                        if key[0] != "T":
                            hop(key)
                        elif 0 <= s < B:
                            for stage in range(2):
                                normalise(key, stage)
                    if 0 <= s + 1 < SLOTS:
                        for stage, step in enumerate(SPLIT_MAXIMA[regime(s)]):
                            if step == h:
                                split_maxima(s + 1, stage)
                    if s >= 1 and layer(s - 1) == 0:
                        for step, done in ((IP_NORMS, image_norms), (IP_LOGITS, image_logits),
                                           (IP_WEIGHTS, image_weights)):
                            if h == step:
                                done(s - 1)
                if s == 2 * B + 1:
                    mark_segments(3, ((2, 4),))

        @block.gpsimd
        def _(pool):
            steps = [0]

            def link(ins):
                steps[0] += 1
                ins.then_inc(pool_step, 1)
                pool.wait_ge(pool_step, steps[0])

            nc.gpsimd.memset(ones[:], 1.0).then_inc(ones_ready, 1)
            for v in (vals_wide, vals_mid):
                nc.gpsimd.memset(v[:], 0.0).then_inc(vals_zeroed, 1)
            nc.gpsimd.memset(textip[:, 0:NTEXT], 0.0).then_inc(ones_ready, 1)

            def lower_parts(key):
                kind, s = key[0], key[1]
                i = plan.split[key]
                pool.wait_ge(rest_ready, i + 1)
                parts = (ksplit if kind == "K" else qsplit)[:].rearrange("p h a t -> p a h t")
                _, middle, low = PARTS[kind]
                nc.gpsimd.tensor_tensor(parts[:, low], rest[:], parts[:, middle], ALU.subtract)\
                    .then_inc(split_ready, 1)

            tt = nc.gpsimd.tensor_tensor

            def steer(s, h):
                n = s * H + h
                if h == POOL_HEADS - 1:
                    taken(pool, ("SEMT", s))
                i = steered_before(n, True)
                pool.wait_ge(pool_copied, i + 1)
                scores = steered[:, n // POOL_HEADS % 2]
                tt(scores, scores, semk[:, s % 3], ALU.add).then_inc(st_steered[1], 1)

            def image_sum(s, stage):
                qt, add = divmod(stage, 2)
                if stage == 0:
                    pool.wait_ge(weights_ready, s + 1)
                    pool.wait_ge(v_ip_loaded[s % 2], 16 * (s // 2 + 1))
                if not add:
                    link(tt(ipprod[:].rearrange("p n (h d) -> p n h d", h=H),
                            v_ip[:, s % 2].rearrange("p n (h d) -> p n h d", h=H),
                            fused[:, 0, qt].rearrange("p h n -> p n h").unsqueeze(3).broadcast_to([P, NIP0, H, D]),
                            ALU.mult))
                    return
                link(tt(ipprod[:, 0:2], ipprod[:, 0:2], ipprod[:, 2:4], ALU.add))
                link(tt(ipprod[:, 0], ipprod[:, 0], ipprod[:, 1], ALU.add))
                ins = tt(attn[:, qt], ipprod[:, 0], attn[:, qt], ALU.add)
                if qt < QT - 1:
                    link(ins)
                else:
                    ins.then_inc(attn_ready, 1)

            def sum_softmaxes(key):
                _, s, rnd, qt = key
                l = layer(s)
                parts = softmaxes(key)
                heads = parts.shape[1]
                h0 = t_rounds(l)[rnd][0] * P // HROWS[l]
                out = attn[:, qt, h0 * D:(h0 + heads) * D].rearrange("p (h d) -> p h d", h=heads)
                taken(pool, key)
                if l == 1:
                    link(nc.gpsimd.tensor_scalar(parts[:, :, 1], parts[:, :, 1], spatial[:, qt:qt + 1], None, ALU.mult))
                if l == 3:
                    link(tt(parts[:, :, 0:2], parts[:, :, 0:2], parts[:, :, 2:4], ALU.add))
                ins = tt(out, parts[:, :, 0], parts[:, :, 1], ALU.add)
                last = (rnd, qt) == (len(t_rounds(l)) - 1, QT - 1)
                ins.then_inc(attn_ready if last else summed, 1)

            for s in range(FIRST, LAST + 1):
                image = s >= 1 and layer(s - 1) == 0
                for h in range(H):
                    if steered_by_pool(s * H + h):
                        steer(s, h)
                    for key in hops_at(s * H + h - 2):
                        if key in plan.split:
                            lower_parts(key)
                        elif key[0] == "T" and layer(key[1]) > 0:
                            sum_softmaxes(key)
                    if image and 0 <= h - IP_WEIGHTS < 4:
                        image_sum(s - 1, h - IP_WEIGHTS)
                if s == 2 * B:
                    pool.wait_ge(o_full, B * QUADS)
                    nc.gpsimd.memset(vals_wide[:], 0.0).then_inc(vals_zeroed, 1)


def kernel(**inputs):
    import ml_dtypes
    import numpy as np
    import concourse.bacc as bacc
    from concourse.bass_utils import run_bass_kernel_spmd as run

    f = lambda name: np.asarray(inputs[name])

    def by_half(w):
        return w.reshape(w.shape[0], NS, 2, D).transpose(0, 2, 3, 1).reshape(w.shape[0], C)

    def rows(w):
        n = HALF if w.shape[0] == C else P
        return w.reshape(-1, n, w.shape[1]).transpose(1, 0, 2)

    names = [
        dict(q="L0_xattn_W_q", k=["L0_xattn_W_k", "L0_xattn_W_k_ip"], v=["L0_xattn_W_v", "L0_xattn_W_v_ip"],
             o="L0_xattn_W_out", b="L0_xattn_b_out"),
        dict(q="L1_xattn_Wq", k=["L1_xattn_Wk", "L1_xattn_Wk_ip"], v=["L1_xattn_Wv", "L1_xattn_Wv_ip"],
             o="L1_xattn_Wout", b="L1_xattn_bout"),
        dict(q="L2_xattn_Wq", k=["L2_xattn_Wk", "L2_xattn_Wk_ip"], v=["L2_xattn_Wv", "L2_xattn_Wv_ip"],
             o="L2_xattn_Wo", b="L2_xattn_bo"),
        dict(q="L3_xattn_to_q_w", k=[f"L3_xattn_to_k_{x}w" for x in ("", "object_", "others_", "ip_")],
             v=[f"L3_xattn_to_v_{x}w" for x in ("", "object_", "others_", "ip_")],
             o="L3_xattn_to_out_w", b="L3_xattn_to_out_b"),
    ]
    w = lambda l, name: f(name).T if l == 2 else f(name)
    arrays = {
        "xT": f("x").reshape(B * S, 2, HALF).transpose(2, 1, 0),
        "ctxT": f("ctx_2048").reshape(B * T, 2, P).transpose(2, 1, 0),
        "text": f("ctx_2048").reshape(B * KT, P, E).transpose(1, 0, 2),
        "spatial": f("fside_S_0").reshape(QT, P).T,
        "wq": np.stack([rows(by_half(w(l, n["q"]))) for l, n in enumerate(names)], 1),
        "wo": np.stack([rows(w(l, n["o"])) for l, n in enumerate(names)], 1),
        "bo": np.stack([f(n["b"]).reshape(2, HALF).T for n in names], 1),
    }
    for l, n in enumerate(names):
        arrays[f"wk{l}"] = np.stack([rows(by_half(w(l, x))) for x in n["k"]], 1)
        arrays[f"wv{l}"] = np.stack([rows(w(l, x)) for x in n["v"]], 1)
    masks = np.zeros((P, 3, KT, 4), np.float32)
    for l in (0, 1, 3):
        marks = np.zeros((len(SEGS[l]), T), np.float32)
        for g, (a, z) in enumerate(SEGS[l]):
            marks[g, a:z] = 1
            masks[:, PATTERN[l], :, g] = marks[g].reshape(KT, P).T
        arrays[f"marks{PATTERN[l]}"] = np.tile(marks, (3, NS)).astype(ml_dtypes.bfloat16)
    arrays["segmask"] = masks
    arrays["ident"] = np.eye(P, dtype=np.float32)
    arrays["identb"] = np.eye(P, dtype=np.float32).astype(ml_dtypes.bfloat16)

    nc = bacc.Bacc("TRN2", target_bir_lowering=False, num_devices=1)
    arrays = {f"in_{k}": np.ascontiguousarray(a) for k, a in arrays.items()}
    t = {k[3:]: nc.dram_tensor(k, a.shape, mybir.dt.from_np(a.dtype), kind="ExternalInput").ap()
         for k, a in arrays.items()}
    t["out"] = nc.dram_tensor("out", (HALF, 2, B * S), F32, kind="ExternalOutput").ap()
    program(nc, t)
    r = run(nc, [arrays], core_ids=[0])
    return r.results[0]["out"].transpose(2, 1, 0).reshape(B, S, C)
```
